# Optimizing a Trainium2 kernel written in Bass

```python
import numpy as np
import jax
import jax.numpy as jnp

def _softmax(x, axis=-1):
    return jax.nn.softmax(x, axis=axis)

def _gelu(x):
    return jax.nn.gelu(x, approximate=True)

def _silu(x):
    return jax.nn.silu(x)

def _sigmoid(x):
    return jax.nn.sigmoid(x)

def _layernorm(x, axis=-1, eps=1e-05):
    m = jnp.mean(x, axis=axis, keepdims=True)
    v = jnp.var(x, axis=axis, keepdims=True)
    return (x - m) / jnp.sqrt(v + eps)

def _scatter_add(tgt, idx, src, axis=0):
    return tgt.at[idx].add(src)

def _segment_sum(src, seg, n):
    return jax.ops.segment_sum(src, seg, n)
kernel_name = 'mk_seq_postln_d1_jaxref_r4_db0c2b'

def setup_inputs(seed: int=0):
    np.random.seed(seed)
    _w = jnp.asarray

    def _L0_attn_setup():
        import math
        import jax, jax.numpy as jnp
        import numpy as np
        HID = 512
        H = 16
        HKV = 8
        D = HID // H
        F = D
        SEQ = 512
        BATCH = 2
        THETA = 10000.0

        def _rotate_half(x):
            x1, x2 = (x[..., :x.shape[-1] // 2], x[..., x.shape[-1] // 2:])
            return jnp.concatenate((-x2, x1), axis=-1)

        def _softmax_kernel(x, R):
            n = jnp.sqrt(jnp.sum(x * x, axis=-1, keepdims=True))
            x = x / jnp.maximum(n, 1e-06)
            p = jnp.einsum('...d,ed->...e', x, R)
            feats = jnp.concatenate([jnp.sin(p), jnp.cos(p)], axis=-1)
            return feats / math.sqrt(F)
        key = jax.random.key(seed)
        ks = jax.random.split(key, 10)
        s = lambda k, shape, scale=0.02: jax.random.normal(k, shape, dtype=jnp.float32) * scale
        return {'hidden_states': jax.random.normal(ks[0], (BATCH, SEQ, HID), dtype=jnp.float32), 'Wq': s(ks[1], (HID, HID)), 'bq': s(ks[2], (HID,)), 'Wk': s(ks[3], (HKV * D, HID)), 'bk': s(ks[4], (HKV * D,)), 'Wv': s(ks[5], (HKV * D, HID)), 'bv': s(ks[6], (HKV * D,)), 'Wo': s(ks[7], (HID, HID)), 'bo': s(ks[8], (HID,)), 'rand_matrix': jax.random.normal(ks[9], (F // 2, D), dtype=jnp.float32)}
    _L0_attn_in = _L0_attn_setup()

    def _L0_ffn_setup():
        import jax, jax.numpy as jnp
        import numpy as np
        BLOCK_SIZE = 32
        HIDDEN_SIZE = 512
        MLP_DIM = 4096
        NVFP4_LUT = jnp.array([0.0, 0.5, 1.0, 1.5, 2.0, 3.0, 4.0, 6.0, 0.0, -0.5, -1.0, -1.5, -2.0, -3.0, -4.0, -6.0], dtype=jnp.float32)

        def dequant_nvfp4(W_packed, scales, block=BLOCK_SIZE):
            N = W_packed.shape[0]
            low = W_packed & 15
            high = W_packed >> 4 & 15
            idx = jnp.stack([low, high], axis=-1).reshape(N, -1)
            vals = NVFP4_LUT[idx]
            K = vals.shape[1]
            vals = vals.reshape(N, K // block, block) * scales[:, :, None]
            return vals.reshape(N, K)
        key = jax.random.key(seed)
        ks = jax.random.split(key, 7)
        x = jax.random.normal(ks[0], (4, 32, HIDDEN_SIZE), dtype=jnp.float32)
        gate_W_packed = jax.random.randint(ks[1], (MLP_DIM, HIDDEN_SIZE // 2), 0, 64, dtype=jnp.int32)
        gate_scales = jax.random.uniform(ks[2], (MLP_DIM, HIDDEN_SIZE // BLOCK_SIZE), dtype=jnp.float32) * 0.1 + 0.001
        up_W_packed = jax.random.randint(ks[3], (MLP_DIM, HIDDEN_SIZE // 2), 0, 64, dtype=jnp.int32)
        up_scales = jax.random.uniform(ks[4], (MLP_DIM, HIDDEN_SIZE // BLOCK_SIZE), dtype=jnp.float32) * 0.1 + 0.001
        down_W_packed = jax.random.randint(ks[5], (HIDDEN_SIZE, MLP_DIM // 2), 0, 64, dtype=jnp.int32)
        down_scales = jax.random.uniform(ks[6], (HIDDEN_SIZE, MLP_DIM // BLOCK_SIZE), dtype=jnp.float32) * 0.1 + 0.001
        return {'x': x, 'gate_W_packed': gate_W_packed, 'gate_scales': gate_scales, 'up_W_packed': up_W_packed, 'up_scales': up_scales, 'down_W_packed': down_W_packed, 'down_scales': down_scales}
    _L0_ffn_in = _L0_ffn_setup()
    _d = {'L0_attn_hidden_states': _L0_attn_in['hidden_states'], 'L0_attn_Wq': _L0_attn_in['Wq'], 'L0_attn_bq': _L0_attn_in['bq'], 'L0_attn_Wk': _L0_attn_in['Wk'], 'L0_attn_bk': _L0_attn_in['bk'], 'L0_attn_Wv': _L0_attn_in['Wv'], 'L0_attn_bv': _L0_attn_in['bv'], 'L0_attn_Wo': _L0_attn_in['Wo'], 'L0_attn_bo': _L0_attn_in['bo'], 'L0_attn_rand_matrix': _L0_attn_in['rand_matrix'], 'L0_ffn_gate_W_packed': _L0_ffn_in['gate_W_packed'], 'L0_ffn_gate_scales': _L0_ffn_in['gate_scales'], 'L0_ffn_up_W_packed': _L0_ffn_in['up_W_packed'], 'L0_ffn_up_scales': _L0_ffn_in['up_scales'], 'L0_ffn_down_W_packed': _L0_ffn_in['down_W_packed'], 'L0_ffn_down_scales': _L0_ffn_in['down_scales']}
    _x0 = _d['L0_attn_hidden_states']
    _d['L0_attn_hidden_states'] = jax.random.normal(jax.random.fold_in(jax.random.key(seed), 1), (2, 2048, 512), dtype=_x0.dtype)
    del _x0
    return _d

def reference(L0_attn_hidden_states, L0_attn_Wq, L0_attn_bq, L0_attn_Wk, L0_attn_bk, L0_attn_Wv, L0_attn_bv, L0_attn_Wo, L0_attn_bo, L0_attn_rand_matrix, L0_ffn_gate_W_packed, L0_ffn_gate_scales, L0_ffn_up_W_packed, L0_ffn_up_scales, L0_ffn_down_W_packed, L0_ffn_down_scales):

    def _L0_attn_ref(hidden_states, Wq, bq, Wk, bk, Wv, bv, Wo, bo, rand_matrix):
        import math
        import jax, jax.numpy as jnp
        import numpy as np
        HID = 512
        H = 16
        HKV = 8
        D = HID // H
        F = D
        SEQ = 512
        BATCH = 2
        THETA = 10000.0

        def _rotate_half(x):
            x1, x2 = (x[..., :x.shape[-1] // 2], x[..., x.shape[-1] // 2:])
            return jnp.concatenate((-x2, x1), axis=-1)

        def _softmax_kernel(x, R):
            n = jnp.sqrt(jnp.sum(x * x, axis=-1, keepdims=True))
            x = x / jnp.maximum(n, 1e-06)
            p = jnp.einsum('...d,ed->...e', x, R)
            feats = jnp.concatenate([jnp.sin(p), jnp.cos(p)], axis=-1)
            return feats / math.sqrt(F)
        b, s, _ = hidden_states.shape
        q = (hidden_states @ Wq.T + bq).reshape(b, s, H, D).transpose(0, 2, 1, 3)
        k = (hidden_states @ Wk.T + bk).reshape(b, s, HKV, D).transpose(0, 2, 1, 3)
        v = (hidden_states @ Wv.T + bv).reshape(b, s, HKV, D).transpose(0, 2, 1, 3)
        inv_freq = 1.0 / THETA ** (jnp.arange(0, D, 2, dtype=jnp.float32) / D)
        freqs = jnp.arange(s, dtype=jnp.float32)[:, None] * inv_freq[None, :]
        emb = jnp.concatenate((freqs, freqs), axis=-1)
        cos = jnp.cos(emb)[None, None, :, :]
        sin = jnp.sin(emb)[None, None, :, :]
        q = q * cos + _rotate_half(q) * sin
        k = k * cos + _rotate_half(k) * sin
        rep = H // HKV
        k = jnp.repeat(k, rep, axis=1)
        v = jnp.repeat(v, rep, axis=1)
        qp = _softmax_kernel(q, rand_matrix)
        kp = _softmax_kernel(k, rand_matrix)
        kv = jnp.einsum('bhsf,bhsd->bsfd', kp, v)
        out = jnp.einsum('bhsf,bsfd->bhsd', qp, kv)
        out = out.reshape(b, s, HID)
        return out @ Wo.T + bo

    def _L0_ffn_ref(x, gate_W_packed, gate_scales, up_W_packed, up_scales, down_W_packed, down_scales):
        import jax, jax.numpy as jnp
        import numpy as np
        BLOCK_SIZE = 32
        HIDDEN_SIZE = 512
        MLP_DIM = 4096
        NVFP4_LUT = jnp.array([0.0, 0.5, 1.0, 1.5, 2.0, 3.0, 4.0, 6.0, 0.0, -0.5, -1.0, -1.5, -2.0, -3.0, -4.0, -6.0], dtype=jnp.float32)

        def dequant_nvfp4(W_packed, scales, block=BLOCK_SIZE):
            N = W_packed.shape[0]
            low = W_packed & 15
            high = W_packed >> 4 & 15
            idx = jnp.stack([low, high], axis=-1).reshape(N, -1)
            vals = NVFP4_LUT[idx]
            K = vals.shape[1]
            vals = vals.reshape(N, K // block, block) * scales[:, :, None]
            return vals.reshape(N, K)
        B, S, H = x.shape
        xt = x.reshape(B * S, H)
        Wg = dequant_nvfp4(gate_W_packed, gate_scales)
        Wu = dequant_nvfp4(up_W_packed, up_scales)
        Wd = dequant_nvfp4(down_W_packed, down_scales)
        gate = jnp.einsum('th,nh->tn', xt, Wg)
        up = jnp.einsum('th,nh->tn', xt, Wu)
        gelu = jnp.tanh(0.7978845608028654 * (gate + 0.044715 * gate ** 3)) * gate * 0.5 + gate * 0.5
        inter = gelu * up
        out = jnp.einsum('tn,hn->th', inter, Wd)
        return out.reshape(B, S, H)
    x = L0_attn_hidden_states
    x = _layernorm(x + _L0_attn_ref(x, L0_attn_Wq, L0_attn_bq, L0_attn_Wk, L0_attn_bk, L0_attn_Wv, L0_attn_bv, L0_attn_Wo, L0_attn_bo, L0_attn_rand_matrix), axis=-1)
    x = _layernorm(x + _L0_ffn_ref(x, L0_ffn_gate_W_packed, L0_ffn_gate_scales, L0_ffn_up_W_packed, L0_ffn_up_scales, L0_ffn_down_W_packed, L0_ffn_down_scales), axis=-1)
    return x

_drawn_inputs = setup_inputs


def setup_inputs(seed=0):
    import zlib

    import numpy as np

    out = dict(_drawn_inputs(seed))
    spreads = {}
    factors = {'L0_attn_bq': 8.0, 'L0_attn_bk': 8.0, 'L0_attn_bv': 4.005}
    for name, (base, spread) in spreads.items():
        noise = np.random.default_rng([zlib.crc32(name.encode()), seed]).standard_normal(out[name].shape)
        drawn = base * np.exp(spread * noise) if base else spread * noise
        out[name] = jnp.asarray(drawn.astype(out[name].dtype))
    for name, factor in factors.items():
        out[name] = (out[name] * factor).astype(out[name].dtype)
    return out
```

```python
from contextlib import ExitStack

import concourse.bass as bass
from concourse import mybir

ALU = mybir.AluOpType
ACT = mybir.ActivationFunctionType
AX = mybir.AxisListType
F32 = mybir.dt.float32
F16 = mybir.dt.float16
I32 = mybir.dt.int32
U16 = mybir.dt.uint16
ds = bass.ds

P = 128
HID = 512
HEADS = 16
KV_HEADS = 8
D = HID // HEADS
E = D // 2
BATCH = 2
SEQ = 2048
TOKENS = BATCH * SEQ
MLP = 4096

TB = 512
BLOCKS = TOKENS // TB
GROUP = HEADS // KV_HEADS
TT = TB // P
TILES = TOKENS // P
KT = HID // P
KVW = KV_HEADS * D
QKV = HID + 2 * KVW

CH = 512
CHUNKS = MLP // CH
NT = CH // P
STEPS = CHUNKS * BLOCKS
AW = (KV_HEADS + HEADS) * E
HH = HEADS // 2
UPB = 2 * TT
WCH = 3 * 2 * CH
UNITS = 8
UC = WCH // UNITS
HALVES = ((0, 0), (0, 1), (1, 0))

W_SCALE = 256.0
O_SCALE = 64.0
BO_SCALE = 128.0
X1_SCALE = 1024.0
FFN_SCALE = 256.0
INTER_SCALE = 0.25
FP4_BITS = 2.0 ** 14
LN_EPS = 1e-5
NORM_EPS = 1e-6
TWO_PI = 6.283185307179586
HALF_TURN = 3.1415925
ROUND = 1.5 * 2.0 ** 23
GELU_C = 0.7978845608028654
GELU_A = 0.044715
RSQRT_SEED = float(0x5F3759DF)

C_IDENT = 0
C_ONES4 = C_IDENT + P
C_SIGN = C_ONES4 + 4
C_BIAS = C_SIGN + 1
C_SCALE = C_BIAS + 6
C_END = C_SCALE + P

JOBS = (("k0", 0), ("k1", 128), ("q0", 256), ("q1", 384), ("q2", 512), ("q3", 640), ("v0", 768), ("v1", 768))
QK = 6
LOAD_ORDER = (2, 3, 0, 1)
JB = 3


class Own:

    def __init__(self, eng, sem, base):
        self.eng, self.sem, self.base, self.n = eng, sem, base, 0

    def tick(self, ins):
        ins.then_inc(self.sem, 1)
        self.n += 1

    def wait(self):
        self.eng.wait_ge(self.sem, self.base + self.n)

    def done(self, ins):
        self.tick(ins)
        self.wait()


def build(nc, xblk, x, wqkv_d, wo_d, r_d, consts_d, bv_d, bo_d, tables_d, codes_d, scales_d, out):
    with ExitStack() as ctx:
        def sb(name, cols, dt=F32):
            return ctx.enter_context(nc.sbuf_tensor(name, [P, cols], dt))

        def sem(name):
            return ctx.enter_context(nc.semaphore(name))

        XB = 2 * KT * TB
        XT = sb("XT", BLOCKS * XB, F16)
        ACC = sb("ACC", TILES * HID)
        WPAR = 2 * 2 * WCH
        WB = sb("WB", 2 * WPAR, F16)
        T2 = sb("T2", 5088)
        DQ = sb("DQ", 2560)

        def carve(t, off, cols, dt=F32):
            size = 2 if t.dtype == F16 else 4
            nbytes = cols * (2 if dt in (F16, U16) else 4)
            v = t[:, off // size:(off + nbytes) // size]
            return v if t.dtype == dt else v.bitcast(dt)

        def xt(i, half, kt, lo=0, n=TB):
            return XT[:, ds(i * XB + ((half * KT + kt) * TB + lo), n)]

        def xt_half(i, half):
            return XT[:, ds(i * XB + half * KT * TB, KT * TB)].rearrange("p (k n) -> p k n", k=KT)

        def acc(i, tt):
            return ACC[:, ds(i * (TT * HID) + tt * HID, HID)]

        def weight(par, m, kt, half, lo, n):
            return WB[:, ds(par + ((kt % 2) * 2 * WCH + half * WCH + (m * 2 + kt // 2) * CH + lo), n)]

        wqkv = carve(WB, 0, 2 * KT * QKV, F16).rearrange("p (h k n) -> p h k n", h=2, k=KT)
        wo = carve(WB, 16384, 2 * KT * HID, F16).rearrange("p (h k n) -> p h k n", h=2, k=KT)
        ang = carve(WB, 24576, 2 * TT * AW)
        v = carve(WB, 36864, TT * KVW).rearrange("p (t n) -> p t n", t=TT)
        xtile = carve(WB, 40960, TT * HID).rearrange("p (t n) -> p t n", t=TT)
        ring = carve(ACC, 0, QK * 3 * TB).rearrange("p (s c n) -> p s c n", s=QK, c=3)
        xs = carve(ACC, 36864, KT * TB)
        dif = [carve(ACC, 45056 + 4096 * n, HH * KV_HEADS * E) for n in range(2)]
        prod = [carve(ACC, 53248, HH * D * KV_HEADS), carve(DQ, 0, HH * D * KV_HEADS)]
        wraw = carve(ACC, 0, KT * QKV).rearrange("p (k n) -> p k n", k=KT)
        woraw = carve(ACC, 45056, KT * HID).rearrange("p (k n) -> p k n", k=KT)
        cst = carve(T2, 0, C_END)
        rdir = carve(T2, 1600, 2 * 4 * E).rearrange("p (c n) -> p c n", c=2)
        bv = carve(T2, 2112, KVW)
        tab = carve(T2, 3136, 2 * TB).rearrange("p (c n) -> p c n", c=2)
        small = carve(T2, 7232, 128)
        oT = carve(T2, 7744, 2 * 2 * KT * P, F16).rearrange("p (b s k n) -> p b s k n", b=2, s=2, k=KT)
        score = carve(T2, 11840, 2 * HH * KV_HEADS).rearrange("p (b n) -> p b n", b=2)
        turns = carve(T2, 12352, AW)
        o = [carve(t, at, TT * HH * D).rearrange("p (h t d) -> p h t d", h=HH, t=TT) for t, at in ((T2, 13888), (ACC, 61440))]
        bo = carve(DQ, 8192, HID)
        bo_halves = carve(T2, 17984, 2 * HID + P, F16)
        gbuf = carve(T2, 0, 2 * TB).rearrange("p (b n) -> p b n", b=2)
        zbuf = carve(T2, 4096, 2 * TB).rearrange("p (b n) -> p b n", b=2)
        inter = carve(T2, 8192, 4 * 2 * TB // 2).bitcast(F16).rearrange("p (s h n) -> p s h n", s=4, h=2)
        stat = carve(T2, 16384, 64)
        raw = carve(DQ, 0, UC, I32)
        scl = carve(DQ, 1536, UC)
        c16 = carve(DQ, 3072, UC, U16)
        mag = carve(DQ, 3840, UC, U16)
        sgn = carve(DQ, 4608, UC, U16)
        w32 = carve(DQ, 5376, UC)
        total = carve(DQ, 0, TT * HID).rearrange("p (t n) -> p t n", t=TT)

        ident = cst[:, C_IDENT:C_IDENT + P]
        norms = small[:, 64:112].rearrange("p (b n) -> p b n", b=2)
        ln_eps, biases, scratch = small[:, 112:113], small[:, 113:119], small[:, 120:121]

        def stats(tt):
            return small[:, 16 * tt:16 * tt + 16]

        x1_d = nc.dram_tensor("x1_scratch", (TT, 2 + BLOCKS, P, HID), F32).ap()

        bank = [ctx.enter_context(nc.psum_tensor(f"bank{b}", [P, 512], F32))[:, :] for b in range(8)]
        job, feat, otp, att, trp = bank[0:JB], bank[3:5], bank[5], bank[6], bank[7]
        gate, up, down = bank[0:2], bank[2:4], bank[4:8]

        constants_loaded = sem("constants_loaded")
        wraw_loaded = sem("wraw_loaded")
        wqkv_hi = sem("wqkv_hi")
        wqkv_lo = sem("wqkv_lo")
        prepared = sem("prepared")
        bo_hi = sem("bo_hi")
        wo_hi = sem("wo_hi")
        wo_lo = sem("wo_lo")
        x_loaded = sem("x_loaded")
        x_hi = sem("x_hi")
        x_lo = sem("x_lo")
        tab_loaded = sem("tab_loaded")
        job_ready = sem("job_ready")
        job_used = sem("job_used")
        squared = sem("squared")
        feat_ready = sem("feat_ready")
        norm_ready = sem("norm_ready")
        feat_used = sem("feat_used")
        ang_ready = sem("ang_ready")
        dif_ready = sem("dif_ready")
        sin_ready = sem("sin_ready")
        sin2_ready = sem("sin2_ready")
        score_ready = sem("score_ready")
        prod_ready = sem("prod_ready")
        o_ready = sem("o_ready")
        ot_ready = sem("ot_ready")
        ot_hi = sem("ot_hi")
        ot_lo = sem("ot_lo")
        xtile_loaded = [sem(f"xtile_loaded_{tt}") for tt in range(TT)]
        att_ready = sem("att_ready")
        moments_taken = sem("moments_taken")
        var_ready = sem("var_ready")
        std_ready = sem("std_ready")
        inverse_ready = sem("inverse_ready")
        x1_ready = sem("x1_ready")
        x1_stored = [sem(f"x1_stored_{tt}") for tt in range(TT)]
        acc_loaded = sem("acc_loaded")
        tr_ready = sem("tr_ready")
        x1_hi = sem("x1_hi")
        x1_lo = sem("x1_lo")
        codes_loaded = sem("codes_loaded")
        scales_loaded = sem("scales_loaded")
        c16_ready = sem("c16_ready")
        w32_ready = sem("w32_ready")
        weight_hi = sem("weight_hi")
        weight_lo = sem("weight_lo")
        gate_ready = sem("gate_ready")
        gate_copied = sem("gate_copied")
        gate_squared = sem("gate_squared")
        z_ready = sem("z_ready")
        tanh_ready = sem("tanh_ready")
        up_ready = sem("up_ready")
        inter_ready = sem("inter_ready")
        inter_hi = sem("inter_hi")
        inter_lo = sem("inter_lo")
        down_ready = sem("down_ready")
        down_added = sem("down_added")
        out_ready = sem("out_ready")
        out_written = sem("out_written")
        own_early = sem("vector_own_early")
        own_late = sem("vector_own_late")
        own_dq = sem("vector_own_dequant")
        own_ffn = sem("vector_own_ffn")
        own_ln = sem("vector_own_layernorm")
        OWN_EARLY, OWN_LATE, OWN_DQ, OWN_FFN, OWN_LN = 3 * TT, UPB, 6, 2 * NT, 20

        block = ctx.enter_context(nc.Block())

        def ge(eng, semaphore, value):
            if not isinstance(value, int) or value > 0:
                eng.wait_ge(semaphore, value)

        def attention_blocks(eng, body):
            body(0, None, None, True)
            body(1, 0, None, True)
            with eng.Fori(2, BLOCKS - 1) as i:
                body(i, i - 1, i - 2, True)
            body(BLOCKS - 1, BLOCKS - 2, BLOCKS - 3, False)
            body(None, BLOCKS - 1, BLOCKS - 2, False)
            body(None, None, BLOCKS - 1, False)

        def in_order(order, first, second, i, b, c):
            for step, n in order:
                at = i if step in first else b if step in second or n < 2 else c
                if at is not None:
                    step(at, n)

        def first_chunk(eng, unit):
            unit(0)
            with eng.Fori(1, UNITS) as u:
                unit(u)

        def ffn_steps(eng, body, before_sums=None):
            body(0, False, True, False)
            if before_sums:
                before_sums()
            with eng.Fori(1, STEPS - BLOCKS) as g:
                body(g, True, True, False)
            body(STEPS - BLOCKS, True, False, False)
            body(STEPS - BLOCKS + 1, True, False, True)
            with eng.Fori(STEPS - BLOCKS + 2, STEPS) as g:
                body(g, True, False, True)

        @block.sync
        def _(sp):
            sp.dma_start(wraw.rearrange("p k n -> p (k n)"), wqkv_d).then_inc(wraw_loaded, 16)
            sp.dma_start(cst, consts_d).then_inc(constants_loaded, 16)
            sp.dma_start(rdir.rearrange("p c n -> p (c n)"), r_d).then_inc(constants_loaded, 16)
            sp.dma_start(bv, bv_d.partition_broadcast(P)).then_inc(constants_loaded, 16)
            sp.dma_start(bo, bo_d.partition_broadcast(P)).then_inc(constants_loaded, 16)
            sp.dma_start(woraw.rearrange("p k n -> p (k n)"), wo_d).then_inc(constants_loaded, 16)

            def one(blocks, i):
                if isinstance(i, int):
                    return blocks[i]
                return blocks[ds(i, 1)].rearrange("o p n -> (o p) n")

            def load_x(i, shift=0):
                ge(sp, x_lo, i + shift)
                sp.dma_start(xs, one(xblk[shift:], i)).then_inc(x_loaded, 16)

            def load_table(i, shift=0):
                ge(sp, job_used, len(JOBS) * (i + (shift - 1)) + QK)
                sp.dma_start(tab.rearrange("p c n -> p (c n)"), one(tables_d[shift:], i)).then_inc(tab_loaded, 16)

            def load_tile(i, tt):
                sp.dma_start(xtile[:, tt, :], one(x[LOAD_ORDER.index(tt)], i)).then_inc(
                    xtile_loaded[tt], 16)

            load_x(0)
            load_table(0)
            for tt in range(TT):
                load_tile(0, tt)

            def store_x1(b, tt, at):
                sp.wait_ge(tr_ready, b * TT + (tt + 1))
                sp.dma_start(at, xtile[:, tt, :]).then_inc(x1_stored[tt], 16)

            def body(i, b, c, following):
                if following:
                    load_x(i, 1)
                for tt in (2, 3):
                    if c is not None:
                        store_x1(c, tt, one(x1_d[tt], i) if i is not None else x1_d[tt, 2 + c])
                        if b is not None:
                            sp.wait_ge(x1_stored[tt], 16 * (c + 1))
                            load_tile(b, tt)
                    if following and tt == 2:
                        load_table(i, 1)
                if b is not None:
                    for tt in (0, 1):
                        store_x1(b, tt, one(x1_d[tt, 1:], i) if i is not None else x1_d[tt, 2 + b])
                        if i is not None:
                            sp.wait_ge(x1_stored[tt], 16 * (b + 1))
                            load_tile(i, tt)

            attention_blocks(sp, body)

            def load_codes(u):
                sp.wait_ge(c16_ready, u)
                sp.dma_start(raw, codes_d[ds(u, 1), :, :].rearrange("o p n -> (o p) n")).then_inc(codes_loaded, 16)
                sp.wait_ge(w32_ready, 2 * u)
                sp.dma_start(scl, scales_d[ds(u, 1), :, :].rearrange("o p n -> (o p) n")).then_inc(scales_loaded, 16)

            sp.wait_ge(o_ready, BLOCKS * UPB)
            sp.dma_start(raw, codes_d[0]).then_inc(codes_loaded, 16)
            sp.dma_start(scl, scales_d[0]).then_inc(scales_loaded, 16)
            with sp.Fori(1, UNITS) as u:
                load_codes(u)
            sp.wait_ge(x1_lo, TILES)
            for tt in range(TT):
                sp.wait_ge(x1_stored[tt], 16 * BLOCKS)
            with sp.Fori(0, BLOCKS) as b:
                sp.dma_start(ACC[:, ds(b * (TT * HID), TT * HID)].rearrange("p (t n) -> p t n", t=TT),
                             x1_d[:, 2:][:, ds(b, 1)].rearrange("t o p n -> p (o t) n")).then_inc(acc_loaded, 16)
            with sp.Fori(UNITS, CHUNKS * UNITS) as u:
                load_codes(u)

            with sp.Fori(0, BLOCKS) as b:
                for tt in range(TT):
                    sp.wait_ge(out_ready, b * TT + (tt + 1))
                    sp.dma_start(out[ds(b * TB + tt * P, P), :], total[:, tt, :]).then_inc(out_written, 16)
            sp.wait_ge(out_written, 16 * TILES)

        @block.gpsimd
        def _(pool):
            def difference(b, u):
                n, tt, half = b * UPB + u, u % TT, u // TT
                ge(pool, score_ready, n - 1)
                at = (b & 1) * (TT * AW) + tt * AW
                q = ang[:, ds(at + (KV_HEADS + half * HH) * E, HH * E)]
                k = ang[:, ds(at, KV_HEADS * E)]
                shape = [P, HH, KV_HEADS, E]
                nc.gpsimd.tensor_tensor(
                    dif[u % 2].rearrange("p (h g e) -> p h g e", h=HH, g=KV_HEADS),
                    q.rearrange("p (h e) -> p h e", e=E).unsqueeze(2).to_broadcast(shape),
                    k.rearrange("p (g e) -> p g e", e=E).unsqueeze(1).to_broadcast(shape),
                    ALU.subtract).then_inc(dif_ready, 1)

            def product(b, u):
                n, tt = b * UPB + u, u % TT
                ge(pool, o_ready, n - 1)
                pool.wait_ge(score_ready, n + 1)
                shape = [P, HH, D, KV_HEADS]
                nc.gpsimd.tensor_tensor(
                    prod[u % 2].rearrange("p (h d g) -> p h d g", h=HH, g=KV_HEADS),
                    score[:, u % 2, :].rearrange("p (h g) -> p h g", g=KV_HEADS).unsqueeze(2).to_broadcast(shape),
                    v[:, tt, :].rearrange("p (g d) -> p d g", d=D).unsqueeze(1).to_broadcast(shape),
                    ALU.mult).then_inc(prod_ready, 1)

            POOL_ORDER = (
                (difference, 0), (difference, 1), (difference, 2), (product, 0), (difference, 3), (difference, 4),
                (product, 1), (product, 2), (product, 3), (difference, 5), (product, 4), (difference, 6),
                (product, 5), (difference, 7), (product, 6), (product, 7))

            def body(i, b, c, following):
                if b is not None:
                    pool.wait_ge(ang_ready, (b + 1) * TT)
                    pool.wait_ge(job_used, (b + 1) * len(JOBS))
                    in_order(POOL_ORDER, (), (difference, product), i, b, c)

            pool.wait_ge(wo_lo, KT)
            attention_blocks(pool, body)

            def weight_lo_half(u, nib):
                pool.wait_ge(weight_hi, 2 * u + (nib + 1))
                par = ((u >> 3) & 1) * WPAR
                col = nib * 2 * WCH
                at = par + (u & 7) * UC
                nc.gpsimd.tensor_tensor(WB[:, ds(at + (col + WCH), UC)], w32, WB[:, ds(at + col, UC)],
                                        ALU.subtract).then_inc(weight_lo, 1)

            first_chunk(pool, lambda u: (weight_lo_half(u, 0), weight_lo_half(u, 1)))

            def body(g, add, dequantise, normalise):
                for nt in range(NT):
                    pool.wait_ge(inter_hi, g * NT + (nt + 1))
                    nc.gpsimd.tensor_tensor(inter[:, nt, 1, :], zbuf[:, nt % 2, :], inter[:, nt, 0, :],
                                            ALU.subtract).then_inc(inter_lo, 1)
                    if dequantise and nt >= 2:
                        weight_lo_half(g + UNITS, nt - 2)

            ffn_steps(pool, body)

        @block.scalar
        def _(act):
            for k in range(KT):
                act.wait_ge(wraw_loaded, 16)
                nc.scalar.activation(wqkv[:, 0, k, :], wraw[:, k, :], ACT.Copy, scale=W_SCALE).then_inc(wqkv_hi, 1)

            for k in range(KT):
                act.wait_ge(constants_loaded, 16 * 5)
                nc.scalar.activation(wo[:, 0, k, :], woraw[:, k, :], ACT.Copy, scale=W_SCALE).then_inc(wo_hi, 1)
            act.wait_ge(prepared, 1)

            def square(i, k):
                act.wait_ge(job_ready, i * len(JOBS) + (k + 1))
                ge(act, feat_ready, i * TT)
                nc.scalar.activation(ring[:, k, 2, :], job[k % JB], ACT.Square,
                                     bias=biases[:, k:k + 1]).then_inc(squared, 1)

            def sine(b, u):
                n = b * UPB + (u + 1)
                act.wait_ge(dif_ready, n)
                nc.scalar.activation(dif[u % 2], dif[u % 2], ACT.Sin, scale=HALF_TURN).then_inc(sin_ready, 1)
                act.wait_ge(sin_ready, n)
                nc.scalar.activation(dif[u % 2], dif[u % 2], ACT.Square).then_inc(sin2_ready, 1)

            def turned_hi(b, tt):
                t = b * TT + tt
                act.wait_ge(ot_ready, t + 1)
                ge(act, att_ready, t - 1)
                nc.scalar.activation(oT[:, tt % 2, 0, :, :].rearrange("p k n -> p (k n)"), otp, ACT.Copy,
                                     scale=O_SCALE).then_inc(ot_hi, 1)

            def deviation(b, tt):
                act.wait_ge(var_ready, b * TT + (tt + 1))
                nc.scalar.activation(stats(tt)[:, 8:9], stats(tt)[:, 7:8], ACT.Sqrt, bias=ln_eps).then_inc(std_ready, 1)

            def keep_hi(b, tt):
                act.wait_ge(tr_ready, b * TT + (tt + 1))
                nc.scalar.activation(xt_half(b, 0)[:, :, tt * P:tt * P + P],
                                     trp.rearrange("p (k n) -> p k n", k=KT), ACT.Copy,
                                     scale=X1_SCALE).then_inc(x1_hi, 1)

            def root(i, tt):
                act.wait_ge(feat_ready, i * TT + (tt + 1))
                ge(act, feat_used, i * TT + (tt - 1))
                nc.scalar.activation(norms[:, tt % 2, :], feat[tt % 2][:, AW:AW + KV_HEADS + HEADS],
                                     ACT.Sqrt).then_inc(norm_ready, 1)

            def split_hi(i, n=0):
                act.wait_ge(x_loaded, 16 * (i + 1))
                nc.scalar.activation(XT[:, ds(i * XB, KT * TB)], xs, ACT.Copy).then_inc(x_hi, 1)

            def split_next(i, n):
                split_hi(i + 1)

            SCALAR_ORDER = (
                (sine, 0), (turned_hi, 2), (square, 0), (square, 1), (square, 2), (sine, 1), (sine, 2),
                (split_next, 0), (deviation, 2), (sine, 3), (square, 3), (square, 4), (square, 5), (turned_hi, 3),
                (keep_hi, 2), (root, 0), (sine, 4), (root, 1), (sine, 5), (turned_hi, 0), (deviation, 3),
                (root, 2), (turned_hi, 1), (sine, 6), (keep_hi, 3), (deviation, 0), (sine, 7), (root, 3),
                (deviation, 1), (keep_hi, 0), (keep_hi, 1))

            def body(i, b, c, following):
                order = SCALAR_ORDER if following else [s for s in SCALAR_ORDER if s[0] is not split_next]
                in_order(order, (square, root, split_next), (sine,), i, b, c)

            split_hi(0)
            attention_blocks(act, body)

            def narrow(u):
                act.wait_ge(codes_loaded, 16 * (u + 1))
                ge(act, w32_ready, 2 * u)
                nc.scalar.activation(c16, raw.bitcast(U16).rearrange("p (n two) -> p n two", two=2)[:, :, 0],
                                     ACT.Copy).then_inc(c16_ready, 1)

            def weight_hi_half(u, nib):
                act.wait_ge(w32_ready, 2 * u + (nib + 1))
                at = ((u >> 3) & 1) * WPAR + (u & 7) * UC + nib * 2 * WCH
                nc.scalar.activation(WB[:, ds(at, UC)], w32, ACT.Copy).then_inc(weight_hi, 1)

            act.wait_ge(att_ready, TILES)
            first_chunk(act, lambda u: (narrow(u), weight_hi_half(u, 0), weight_hi_half(u, 1)))

            def body(g, add, dequantise, normalise):
                for nt in range(NT):
                    b = nt % 2
                    act.wait_ge(gate_ready, g * NT + (nt + 1))
                    ge(act, inter_ready, g * NT + (nt - 1))
                    ge(act, inter_lo, g * NT + (nt - 1))
                    nc.scalar.activation(gbuf[:, b, :], gate[b], ACT.Copy,
                                         scale=1.0 / (X1_SCALE * FFN_SCALE)).then_inc(gate_copied, 1)
                    nc.scalar.activation(zbuf[:, b, :], gate[b], ACT.Square,
                                         scale=1.0 / (X1_SCALE * FFN_SCALE)).then_inc(gate_squared, 1)
                    act.wait_ge(z_ready, g * NT + (nt + 1))
                    nc.scalar.activation(zbuf[:, b, :], zbuf[:, b, :], ACT.Tanh, scale=GELU_C).then_inc(tanh_ready, 1)
                    act.wait_ge(inter_ready, g * NT + (nt + 1))
                    if not isinstance(g, int) or g > 0:
                        act.wait_ge(down_ready, g * NT * TT + (nt - NT + 1) * TT)
                    nc.scalar.activation(inter[:, nt, 0, :], zbuf[:, b, :], ACT.Copy).then_inc(inter_hi, 1)
                    if dequantise and nt == 1:
                        narrow(g + UNITS)
                    if dequantise and nt >= 2:
                        if nt == 2:
                            ge(act, down_ready, g * (NT * TT))
                        weight_hi_half(g + UNITS, nt - 2)

            ffn_steps(act, body)

        @block.vector
        def _(dve):
            def split_lo(i):
                dve.wait_ge(x_hi, i + 1)
                nc.vector.tensor_tensor(XT[:, ds(i * XB + KT * TB, KT * TB)], xs, XT[:, ds(i * XB, KT * TB)],
                                        ALU.subtract).then_inc(x_lo, 1)

            dve.wait_ge(constants_loaded, 16 * 5)
            nc.vector.memset(ln_eps, LN_EPS * (O_SCALE * W_SCALE) ** 2)
            nc.vector.tensor_scalar(rdir[:, 1, :], rdir[:, 1, :], cst[:, C_SIGN:C_SIGN + 1], None, ALU.mult)
            nc.vector.memset(bo_halves[0:1, 2 * HID:], O_SCALE * W_SCALE / BO_SCALE)
            nc.vector.tensor_scalar(bo_halves[0:1, 0:HID], bo[0:1, :], BO_SCALE, None, ALU.mult).then_inc(bo_hi, 1)
            dve.wait_ge(bo_hi, 1)
            nc.vector.scalar_tensor_tensor(bo_halves[0:1, HID:2 * HID], bo[0:1, :], BO_SCALE, bo_halves[0:1, 0:HID],
                                           ALU.mult, ALU.subtract)
            nc.vector.tensor_scalar(biases, cst[:, C_BIAS:C_BIAS + 6], W_SCALE, None, ALU.mult).then_inc(prepared, 1)
            dve.wait_ge(prepared, 1)
            for k in range(KT):
                dve.wait_ge(wqkv_hi, k + 1)
                nc.vector.scalar_tensor_tensor(wqkv[:, 1, k, :], wraw[:, k, :], W_SCALE, wqkv[:, 0, k, :],
                                               ALU.mult, ALU.subtract).then_inc(wqkv_lo, 1)

            for k in range(KT):
                dve.wait_ge(wo_hi, k + 1)
                nc.vector.scalar_tensor_tensor(wo[:, 1, k, :], woraw[:, k, :], W_SCALE, wo[:, 0, k, :],
                                               ALU.mult, ALU.subtract).then_inc(wo_lo, 1)
            split_lo(0)
            dve.wait_ge(wqkv_lo, KT)

            def rotate(i, k, own):
                if k == 0:
                    dve.wait_ge(tab_loaded, 16 * (i + 1))
                dve.wait_ge(squared, i * QK + (k + 1))
                ge(dve, feat_ready, i * TT)
                for c in range(2):
                    last = nc.vector.scalar_tensor_tensor(ring[:, k, c, :], job[k % JB], biases[:, k:k + 1],
                                                          tab[:, c, :], ALU.add, ALU.mult)
                last.then_inc(job_used, 1)

            def value(i, pair, own):
                k = QK + pair
                dve.wait_ge(job_ready, i * len(JOBS) + (k + 1))
                ge(dve, prod_ready, i * UPB - 2 * (1 - pair))
                nc.vector.scalar_tensor_tensor(
                    v[:, 2 * pair:2 * pair + 2, :], job[k % JB].rearrange("p (t n) -> p t n", t=2), 1.0 / W_SCALE,
                    bv.unsqueeze(1).to_broadcast([P, 2, KVW]), ALU.mult, ALU.add).then_inc(job_used, 1)

            def normalise(i, tt, own):
                dve.wait_ge(norm_ready, i * TT + (tt + 1))
                r = norms[:, tt % 2, :]
                own.done(nc.vector.tensor_scalar(r, r, NORM_EPS * W_SCALE, TWO_PI, ALU.max, ALU.mult))
                own.done(nc.vector.reciprocal(r, r))
                if tt == 0:
                    ge(dve, dif_ready, (i - 1) * UPB)
                mine = ang[:, ds((i & 1) * (TT * AW) + tt * AW, AW)]
                nc.vector.tensor_tensor(
                    mine.rearrange("p (h e) -> p h e", e=E),
                    feat[tt % 2][:, 0:AW].rearrange("p (h e) -> p h e", e=E),
                    r.unsqueeze(2).to_broadcast([P, KV_HEADS + HEADS, E]), ALU.mult).then_inc(feat_used, 1)
                dve.wait_ge(feat_used, i * TT + (tt + 1))
                own.done(nc.vector.tensor_scalar(turns, mine, ROUND, None, ALU.add))
                nc.vector.scalar_tensor_tensor(mine, turns, ROUND, mine, ALU.subtract, ALU.subtract).then_inc(ang_ready, 1)

            def scores(b, u, own):
                n = b * UPB + u
                dve.wait_ge(sin2_ready, n + 1)
                ge(dve, prod_ready, n - 1)
                own.done(nc.vector.tensor_reduce(score[:, u % 2, :], dif[u % 2].rearrange("p (n e) -> p n e", e=E),
                                                 AX.X, ALU.add))
                nc.vector.tensor_scalar(score[:, u % 2, :], score[:, u % 2, :], -2.0 * GROUP / D, GROUP * E / D,
                                        ALU.mult, ALU.add).then_inc(score_ready, 1)

            def sum_heads(b, u, own):
                n, tt, half = b * UPB + u, u % TT, u // TT
                dve.wait_ge(prod_ready, n + 1)
                ge(dve, ot_ready, b * TT - 2 * (1 - half))
                nc.vector.tensor_reduce(o[half][:, :, tt, :],
                                        prod[u % 2].rearrange("p (h d g) -> p h d g", h=HH, g=KV_HEADS),
                                        AX.X, ALU.add).then_inc(o_ready, 1)

            def turned_lo(b, tt, own):
                dve.wait_ge(ot_hi, b * TT + (tt + 1))
                nc.vector.scalar_tensor_tensor(oT[:, tt % 2, 1, :, :].rearrange("p k n -> p (k n)"), otp, O_SCALE,
                                               oT[:, tt % 2, 0, :, :].rearrange("p k n -> p (k n)"),
                                               ALU.mult, ALU.subtract).then_inc(ot_lo, 1)

            def moments(b, tt, own):
                t1 = b * TT + (tt + 1)
                dve.wait_ge(att_ready, t1)
                nc.vector.bn_stats(stats(tt)[:, 0:6], att).then_inc(moments_taken, 1)
                dve.wait_ge(moments_taken, t1)
                nc.vector.memset(scratch, 0.0)
                nc.vector.bn_aggr(stats(tt)[:, 6:8], stats(tt)[:, 0:6]).then_inc(var_ready, 1)

            def first_norm(b, tt, own):
                dve.wait_ge(std_ready, b * TT + (tt + 1))
                nc.vector.reciprocal(stats(tt)[:, 9:10], stats(tt)[:, 8:9]).then_inc(inverse_ready, 1)
                dve.wait_ge(inverse_ready, b * TT + (tt + 1))
                nc.vector.tensor_scalar(xtile[:, tt, :], att, stats(tt)[:, 6:7], stats(tt)[:, 9:10],
                                        ALU.subtract, ALU.mult).then_inc(x1_ready, 1)

            def keep_lo(b, tt, own):
                dve.wait_ge(x1_hi, b * TT + (tt + 1))
                nc.vector.scalar_tensor_tensor(
                    xt_half(b, 1)[:, :, tt * P:tt * P + P], trp.rearrange("p (k n) -> p k n", k=KT), X1_SCALE,
                    xt_half(b, 0)[:, :, tt * P:tt * P + P], ALU.mult, ALU.subtract).then_inc(x1_lo, 1)

            def split_next(i, n, own):
                split_lo(i + 1)

            VECTOR_ORDER = (
                (scores, 0), (turned_lo, 2), (rotate, 0), (rotate, 1), (scores, 1), (rotate, 2), (scores, 2),
                (moments, 2), (split_next, 0), (first_norm, 2), (sum_heads, 0), (rotate, 3), (rotate, 4),
                (rotate, 5), (scores, 3), (turned_lo, 3), (sum_heads, 1), (normalise, 0), (sum_heads, 2),
                (scores, 4), (sum_heads, 3), (keep_lo, 2), (normalise, 1), (moments, 3), (turned_lo, 0),
                (first_norm, 3), (scores, 5), (sum_heads, 4), (normalise, 2), (keep_lo, 3), (scores, 6),
                (turned_lo, 1), (moments, 0), (value, 0), (first_norm, 0), (sum_heads, 5), (scores, 7),
                (normalise, 3), (moments, 1), (first_norm, 1), (keep_lo, 0), (sum_heads, 6), (value, 1),
                (sum_heads, 7), (keep_lo, 1))

            def body(i, b, c, following):
                early = Own(dve, own_early, 0 if i is None else i * OWN_EARLY)
                late = Own(dve, own_late, 0 if b is None else b * OWN_LATE)
                for step, n in VECTOR_ORDER:
                    if step is split_next and not following:
                        continue
                    if step in (rotate, value, normalise, split_next):
                        if i is not None:
                            step(i, n, early)
                    elif step in (scores, sum_heads) or n < 2:
                        if b is not None:
                            step(b, n, late)
                    elif c is not None:
                        step(c, n, late)
                assert i is None or early.n == OWN_EARLY
                assert b is None or late.n == OWN_LATE

            attention_blocks(dve, body)

            def scaled(u, nib, own):
                if nib == 0:
                    dve.wait_ge(c16_ready, u + 1)
                ge(dve, w32_ready, 2 * u + nib)
                shift = 9 - 4 * nib
                own.done(nc.vector.tensor_scalar(mag, c16, shift, 0x0E00, ALU.logical_shift_left, ALU.bitwise_and))
                own.done(nc.vector.tensor_scalar(sgn, c16, shift + 3, 0x8000, ALU.logical_shift_left, ALU.bitwise_and))
                own.done(nc.vector.tensor_tensor(mag, mag, sgn, ALU.bitwise_or))
                dve.wait_ge(scales_loaded, 16 * (u + 1))
                ge(dve, weight_lo, 2 * u + nib)
                nc.vector.scalar_tensor_tensor(w32, mag.bitcast(F16), FP4_BITS * FFN_SCALE, scl,
                                               ALU.mult, ALU.mult).then_inc(w32_ready, 1)

            def dequantise(u):
                own = Own(dve, own_dq, u * OWN_DQ)
                scaled(u, 0, own)
                scaled(u, 1, own)

            first_chunk(dve, dequantise)

            def add_down(g, last):
                for tt in range(TT):
                    dve.wait_ge(down_ready, g * NT * TT + ((NT - 1) * TT + tt + 1))
                    if last:
                        ge(dve, out_written, ((g - (STEPS - BLOCKS)) * TT) * 16)
                    nc.vector.scalar_tensor_tensor(total[:, tt, :] if last else acc(g & (BLOCKS - 1), tt),
                                                   down[tt], 1.0 / (INTER_SCALE * FFN_SCALE),
                                                   acc(g & (BLOCKS - 1), tt), ALU.mult, ALU.add).then_inc(down_added, 1)

            def second_norm(g):
                own = Own(dve, own_ln, (g - (STEPS - BLOCKS)) * OWN_LN)
                dve.wait_ge(down_added, (g + 1) * TT)
                for tt in range(TT):
                    own.done(nc.vector.bn_stats(stat[:, 6 * tt:6 * tt + 6], total[:, tt, :]))
                nc.vector.memset(stat[:, 44:45], 0.0)
                for tt in range(TT):
                    ins = nc.vector.bn_aggr(stat[:, 24 + 2 * tt:26 + 2 * tt], stat[:, 6 * tt:6 * tt + 6])
                    own.tick(ins)
                own.wait()
                var = stat[:, 24:32].rearrange("p (t two) -> p t two", two=2)[:, :, 1]
                ve, y, t = stat[:, 32:36], stat[:, 36:40], stat[:, 40:44]
                own.done(nc.vector.tensor_scalar(ve, var, LN_EPS, None, ALU.add))
                own.done(nc.vector.tensor_scalar(t.bitcast(I32), ve.bitcast(I32), 1, None, ALU.logical_shift_right))
                own.done(nc.vector.tensor_scalar(y.bitcast(I32), t.bitcast(I32), -1.0, RSQRT_SEED, ALU.mult, ALU.add))
                for _ in range(3):
                    own.done(nc.vector.scalar_tensor_tensor(t, y, -0.5, y, ALU.mult, ALU.mult))
                    own.done(nc.vector.tensor_tensor(t, t, ve, ALU.mult))
                    own.done(nc.vector.scalar_tensor_tensor(y, t, 1.5, y, ALU.add, ALU.mult))
                for tt in range(TT):
                    nc.vector.tensor_scalar(total[:, tt, :], total[:, tt, :], stat[:, 24 + 2 * tt:25 + 2 * tt], y[:, tt:tt + 1],
                                            ALU.subtract, ALU.mult).then_inc(out_ready, 1)
                assert own.n == OWN_LN

            def body(g, add, dequantise, normalise):
                own = Own(dve, own_ffn, g * OWN_FFN)
                own_d = Own(dve, own_dq, (g + UNITS) * OWN_DQ)
                for nt in range(NT):
                    b = nt % 2
                    s1 = g * NT + (nt + 1)
                    dve.wait_ge(gate_squared, s1)
                    own.done(nc.vector.tensor_scalar(zbuf[:, b, :], zbuf[:, b, :], GELU_A, 1.0, ALU.mult, ALU.add))
                    nc.vector.tensor_tensor(zbuf[:, b, :], zbuf[:, b, :], gbuf[:, b, :], ALU.mult).then_inc(z_ready, 1)
                    dve.wait_ge(tanh_ready, s1)
                    own.done(nc.vector.scalar_tensor_tensor(gbuf[:, b, :], zbuf[:, b, :], 1.0, gbuf[:, b, :],
                                                            ALU.add, ALU.mult))
                    dve.wait_ge(up_ready, s1)
                    nc.vector.scalar_tensor_tensor(zbuf[:, b, :], up[b], 0.5 * INTER_SCALE / (X1_SCALE * FFN_SCALE),
                                                   gbuf[:, b, :], ALU.mult, ALU.mult).then_inc(inter_ready, 1)
                    if add and nt == 1:
                        add_down(g - 1, normalise)
                    if dequantise and nt in (1, 2):
                        scaled(g + UNITS, nt - 1, own_d)
                    if normalise and nt == 2:
                        second_norm(g - 1)
                assert own.n == OWN_FFN

            ffn_steps(dve, body, lambda: dve.wait_ge(acc_loaded, 16 * BLOCKS))
            add_down(STEPS - 1, True)
            second_norm(STEPS - 1)

        @block.tensor
        def _(pe):
            pe.wait_ge(prepared, 1)
            pe.wait_ge(wqkv_lo, KT)

            def free(i, k):
                ge(pe, job_used, i * len(JOBS) + ((k - JB + 1) if k >= JB else (-1, 0, -2)[k]))

            def project(i, k):
                _, col = JOBS[k]
                if k == 0:
                    pe.wait_ge(x_lo, i + 1)
                free(i, k)
                for kt in range(KT):
                    for a, b in HALVES:
                        last = nc.tensor.matmul(job[k % JB], wqkv[:, a, kt, col:col + P], xt(i, b, kt),
                                                start=(kt == 0 and a + b == 0), stop=(kt == KT - 1 and a == 1))
                last.then_inc(job_ready, 1)

            def project_v(i, pair):
                k = QK + pair
                _, col = JOBS[k]
                free(i, k)
                for t in range(2):
                    for kt in range(KT):
                        for a, b in HALVES:
                            last = nc.tensor.matmul(job[k % JB][:, t * KVW:(t + 1) * KVW],
                                                    xt(i, a, kt, (2 * pair + t) * P, P), wqkv[:, b, kt, col:col + KVW],
                                                    start=(kt == 0 and a + b == 0), stop=(kt == KT - 1 and a == 1))
                last.then_inc(job_ready, 1)

            def directions(i, tt):
                if tt == 0:
                    pe.wait_ge(job_used, i * len(JOBS) + QK)
                ge(pe, feat_used, i * TT + (tt - 1))
                bank_ = feat[tt % 2]
                for s in range(QK):
                    rows = slice(tt * P, (tt + 1) * P)
                    for c in range(2):
                        nc.tensor.matmul(bank_[:, s * 4 * E:(s + 1) * 4 * E], ring[:, s, c, rows], rdir[:, c, :],
                                         start=(c == 0), stop=(c == 1))
                    last = nc.tensor.matmul(bank_[:, AW + 4 * s:AW + 4 * s + 4], ring[:, s, 2, rows],
                                            cst[:, C_ONES4:C_ONES4 + 4], start=True, stop=True)
                last.then_inc(feat_ready, 1)

            def turn_o(b, tt):
                t = b * TT + tt
                pe.wait_ge(o_ready, b * UPB + TT * (1 + tt // 2))
                ge(pe, ot_lo, t)
                for h in range(KT):
                    last = nc.tensor.transpose(
                        otp.rearrange("p (k h j) -> p k h j", k=KT, h=KT)[:, :, h, :],
                        o[tt // 2][:, tt % 2 * KT + h, :, :].rearrange("p t d -> p (t d)"), ident)
                last.then_inc(ot_ready, 1)

            def project_o(b, tt):
                t = b * TT + tt
                pe.wait_ge(ot_lo, t + 1)
                ge(pe, x1_ready, t)
                for kt in range(KT):
                    for a, h in HALVES:
                        nc.tensor.matmul(att, oT[:, tt % 2, a, kt, :], wo[:, h, kt, :],
                                         start=(kt == 0 and a + h == 0), stop=False)
                for half in range(2):
                    nc.tensor.matmul(att, bo_halves[0:1, 2 * HID:], bo_halves[0:1, half * HID:(half + 1) * HID],
                                     start=False, stop=False)
                pe.wait_ge(xtile_loaded[tt], 16 * (b + 1))
                nc.tensor.matmul(att, cst[:, C_SCALE:C_SCALE + P], xtile[:, tt, :],
                                 start=False, stop=True).then_inc(att_ready, 1)

            def turn_x1(b, tt):
                t = b * TT + tt
                pe.wait_ge(x1_ready, t + 1)
                ge(pe, x1_lo, t)
                for kt in range(KT):
                    lo = (kt // 2) * 2 * P + kt % 2
                    last = nc.tensor.transpose(trp[:, kt * P:(kt + 1) * P], xtile[:, tt, lo:lo + 2 * P - 1:2], ident)
                last.then_inc(tr_ready, 1)

            TENSOR_ORDER = (
                (project, 0), (project, 1), (turn_o, 2), (project, 2), (project_o, 2), (project, 3), (project, 4),
                (project, 5), (turn_o, 3), (turn_x1, 2), (project_v, 0), (directions, 0), (directions, 1),
                (project_o, 3), (turn_o, 0), (directions, 2), (turn_o, 1), (turn_x1, 3), (project_o, 0),
                (directions, 3), (project_o, 1), (turn_x1, 0), (project_v, 1), (turn_x1, 1))

            def body(i, b, c, following):
                in_order(TENSOR_ORDER, (project, project_v, directions), (), i, b, c)

            attention_blocks(pe, body)
            pe.wait_ge(x1_lo, TILES)
            pe.wait_ge(feat_used, TILES)

            def hidden(ps, m, nt, par, b):
                for kt in range(KT):
                    for a, h in HALVES:
                        last = nc.tensor.matmul(ps, weight(par, m, kt, a, nt * P, P), xt(b, h, kt),
                                                start=(kt == 0 and a + h == 0), stop=(kt == KT - 1 and a == 1))
                return last

            def down_product(g, nt):
                b = g & (BLOCKS - 1)
                par = ((g >> 3) & 1) * WPAR
                pe.wait_ge(inter_lo, g * NT + (nt + 1))
                for tt in range(TT):
                    if nt == 0:
                        ge(pe, down_added, g * TT + (tt - TT + 1))
                    for a, h in HALVES:
                        last = nc.tensor.matmul(down[tt], inter[:, nt, a, tt * P:(tt + 1) * P],
                                                weight(par, 2, nt, h, 0, HID),
                                                start=(nt == 0 and a + h == 0), stop=(nt == NT - 1 and a == 1))
                    last.then_inc(down_ready, 1)

            def body(g, add, dequantise, normalise):
                b = g & (BLOCKS - 1)
                par = ((g >> 3) & 1) * WPAR
                pe.wait_ge(weight_lo, ((g >> 3) + 1) * (2 * UNITS))
                for nt in range(NT):
                    s = g * NT + nt
                    ge(pe, gate_squared, s - 1)
                    hidden(gate[nt % 2], 0, nt, par, b).then_inc(gate_ready, 1)
                    ge(pe, inter_ready, s - 1)
                    hidden(up[nt % 2], 1, nt, par, b).then_inc(up_ready, 1)
                    if nt >= 2:
                        down_product(g, nt - 2)
                    elif add:
                        down_product(g - 1, nt + 2)

            ffn_steps(pe, body)
            down_product(STEPS - 1, 2)
            down_product(STEPS - 1, 3)


QUARTERS = BLOCKS // BATCH
ROWS_PH = SEQ // HEADS
ROW_SHAPE = (BATCH, TT, HEADS // TT, QUARTERS, ROWS_PH // QUARTERS, HID)


def by_token(a):
    n = a.shape[-1]
    return a.reshape(-1, TB // 16, 4, TT, n).transpose(0, 3, 2, 1, 4).reshape(-1, TB, n)


def host_constants():
    import numpy as np

    c = np.zeros((P, C_END), np.float32)
    c[:, C_IDENT:C_IDENT + P] = np.eye(P, dtype=np.float32)
    for h in range(4):
        c[D * h:D * h + D, C_ONES4 + h] = 1.0
    c[:, C_SCALE:C_SCALE + P] = np.eye(P, dtype=np.float32) * (O_SCALE * W_SCALE)
    c[:, C_SIGN] = np.where(np.arange(P) % D < E, 1.0, -1.0)
    inv = np.float32(1.0) / np.power(np.float32(10000.0), np.arange(0, D, 2, dtype=np.float32) / np.float32(D))
    freqs = np.arange(SEQ, dtype=np.float32)[:, None] * inv.astype(np.float32)[None, :]
    emb = np.concatenate([freqs, freqs], axis=-1).astype(np.float64)
    emb = by_token(emb)
    tab = np.stack([np.cos(emb), np.sin(emb)]).astype(np.float32)
    tab = np.tile(tab.transpose(1, 3, 0, 2), (1, 4, 1, 1)).reshape(-1, P, 2 * TB)
    return c, np.concatenate([tab] * BATCH)


def kernel(**inputs):
    import numpy as np
    import concourse.bacc as bacc
    from concourse.bass_utils import run_bass_kernel_spmd

    a = {k.split("_", 1)[1]: np.asarray(val) for k, val in inputs.items()}
    x = a["attn_hidden_states"].reshape(TOKENS, HID)
    consts, tables = host_constants()
    consts[:, C_BIAS:C_BIAS + 2] = a["attn_bk"].reshape(2, P).T
    consts[:, C_BIAS + 2:C_BIAS + 6] = a["attn_bq"].reshape(4, P).T
    rt = a["attn_rand_matrix"].T
    rdir = np.zeros((P, 2, 4 * E), np.float32)
    for h in range(4):
        rdir[D * h:D * h + D, 0, h * E:(h + 1) * E] = rt
        rdir[D * h:D * h + D, 1, h * E:(h + 1) * E] = np.concatenate([rt[E:], rt[:E]])
    x_rows = x.reshape(ROW_SHAPE).transpose(1, 0, 3, 2, 4, 5).reshape(TT, BLOCKS, P, HID)[list(LOAD_ORDER)]
    wqkv = np.concatenate([a["attn_Wk"], a["attn_Wq"], a["attn_Wv"]])
    wqkv = wqkv.T.reshape(KT, P, QKV).transpose(1, 0, 2).reshape(P, KT * QKV)
    wo = a["attn_Wo"].T.reshape(KT, P, HID).transpose(1, 0, 2).reshape(P, KT * HID)
    xblk = by_token(x).transpose(0, 2, 1)
    xblk = xblk.reshape(BLOCKS, KT, P, TB).transpose(0, 2, 1, 3).reshape(BLOCKS, P, KT * TB)

    order = np.arange(CH).reshape(2, P, 2).transpose(0, 2, 1).reshape(CH)
    blocks_of = np.arange(2 * P).reshape(2, P) // E
    codes = np.empty((CHUNKS, P, 3, 2, CH), np.int32)
    scales = np.empty((CHUNKS, P, 3, 2, CH), np.float32)
    for c in range(CHUNKS):
        rows = c * CH + order
        for m, name in enumerate(("gate", "up")):
            codes[c, :, m] = a[f"ffn_{name}_W_packed"][rows].reshape(CH, 2, P).transpose(2, 1, 0)
            scales[c, :, m] = a[f"ffn_{name}_scales"][rows][:, blocks_of].transpose(2, 1, 0)
        cols = slice(c * 2 * P, (c + 1) * 2 * P)
        codes[c, :, 2] = a["ffn_down_W_packed"][:, cols].reshape(HID, 2, P).transpose(2, 1, 0)
        scales[c, :, 2] = a["ffn_down_scales"][:, c * CH // 32:][:, blocks_of].transpose(2, 1, 0)
    codes = codes.reshape(CHUNKS, P, UNITS, UC).transpose(0, 2, 1, 3).reshape(CHUNKS * UNITS, P, UC)
    scales = scales.reshape(CHUNKS, P, UNITS, UC).transpose(0, 2, 1, 3).reshape(CHUNKS * UNITS, P, UC)

    arrays = {"xblk": xblk, "x": x_rows, "wqkv": wqkv, "wo": wo, "rdir": rdir.reshape(P, 8 * E), "consts": consts,
              "bv": a["attn_bv"], "bo": a["attn_bo"], "tables": tables, "codes": codes, "scales": scales}
    arrays = {k: np.ascontiguousarray(val) for k, val in arrays.items()}
    nc = bacc.Bacc("TRN2", target_bir_lowering=False, num_devices=1)
    args = [nc.dram_tensor(k, val.shape, mybir.dt.from_np(val.dtype), kind="ExternalInput").ap()
            for k, val in arrays.items()]
    out = nc.dram_tensor("out", (TOKENS, HID), F32, kind="ExternalOutput").ap()
    build(nc, *args, out)
    r = run_bass_kernel_spmd(nc, [arrays], core_ids=[0])
    y = r.results[0]["out"].reshape(BATCH, QUARTERS, TT, HEADS // TT, ROWS_PH // QUARTERS, HID)
    return y.transpose(0, 2, 3, 1, 4, 5).reshape(BATCH, SEQ, HID)
```

```python
from contextlib import ExitStack

import concourse.bass as bass
from concourse import mybir

ALU = mybir.AluOpType
ACT = mybir.ActivationFunctionType
AX = mybir.AxisListType
F32 = mybir.dt.float32
F16 = mybir.dt.float16
I32 = mybir.dt.int32
U16 = mybir.dt.uint16
ds = bass.ds

P = 128
HID = 512
HEADS = 16
KV_HEADS = 8
D = HID // HEADS
E = D // 2
BATCH = 2
SEQ = 2048
TOKENS = BATCH * SEQ
MLP = 4096

TB = 512
BLOCKS = TOKENS // TB
GROUP = HEADS // KV_HEADS
TT = TB // P
TILES = TOKENS // P
KT = HID // P
KVW = KV_HEADS * D
QKV = HID + 2 * KVW

CH = 512
CHUNKS = MLP // CH
NT = CH // P
STEPS = CHUNKS * BLOCKS
AW = (KV_HEADS + HEADS) * E
HH = HEADS // 2
UPB = 2 * TT
VU = 3
WCH = 3 * 2 * CH
UNITS = 8
UC = WCH // UNITS
HIDDEN_UNITS = -(-2 * WCH // 3 // UC)
HALVES = ((0, 0), (0, 1), (1, 0))

W_SCALE = 256.0
O_SCALE = 64.0
BO_SCALE = 128.0
X1_SCALE = 1024.0
FFN_SCALE = 256.0
INTER_SCALE = 0.25
FP4_BITS = 2.0 ** 14
LN_EPS = 1e-5
NORM_EPS = 1e-6
TWO_PI = 6.283185307179586
HALF_TURN = 3.1415925
ROUND = 1.5 * 2.0 ** 23
GELU_C = 0.7978845608028654
GELU_A = 0.044715
RSQRT_SEED = float(0x5F3759DF)

C_IDENT = 0
C_ONES4 = C_IDENT + P
C_SIGN = C_ONES4 + 4
C_BIAS = C_SIGN + 1
C_END = C_BIAS + 6

JOBS = (("k0", 0), ("k1", 128), ("q0", 256), ("q1", 384), ("q2", 512), ("q3", 640), ("v0", 768), ("v1", 768))
QK = 6
LOAD_ORDER = (2, 3, 0, 1)
JB = 3


class Own:

    def __init__(self, eng, sem, base):
        self.eng, self.sem, self.base, self.n = eng, sem, base, 0

    def tick(self, ins):
        ins.then_inc(self.sem, 1)
        self.n += 1

    def wait(self):
        self.eng.wait_ge(self.sem, self.base + self.n)

    def done(self, ins):
        self.tick(ins)
        self.wait()


def build(nc, xblk, x, wqkv_d, wo_d, r_d, consts_d, bv_d, bo_d, tables_d, codes_d, scales_d, out):
    with ExitStack() as ctx:
        def sb(name, cols, dt=F32):
            return ctx.enter_context(nc.sbuf_tensor(name, [P, cols], dt))

        def sem(name):
            return ctx.enter_context(nc.semaphore(name))

        XB = 2 * KT * TB
        XT = sb("XT", BLOCKS * XB, F16)
        ACC = sb("ACC", TILES * HID)
        WPAR = 2 * 2 * WCH
        WB = sb("WB", 2 * WPAR, F16)
        T2 = sb("T2", 5088)
        DQ = sb("DQ", 2560)

        def carve(t, off, cols, dt=F32):
            size = 2 if t.dtype == F16 else 4
            nbytes = cols * (2 if dt in (F16, U16) else 4)
            v = t[:, off // size:(off + nbytes) // size]
            return v if t.dtype == dt else v.bitcast(dt)

        def xt(i, half, kt, lo=0, n=TB):
            return XT[:, ds(i * XB + ((half * KT + kt) * TB + lo), n)]

        def xt_half(i, half):
            return XT[:, ds(i * XB + half * KT * TB, KT * TB)].rearrange("p (k n) -> p k n", k=KT)

        def acc(i, tt):
            return ACC[:, ds(i * (TT * HID) + tt * HID, HID)]

        def weight(par, m, kt, half, lo, n):
            return WB[:, ds(par + ((kt % 2) * 2 * WCH + half * WCH + (m * 2 + kt // 2) * CH + lo), n)]

        wqkv = carve(WB, 0, 2 * KT * QKV, F16).rearrange("p (h k n) -> p h k n", h=2, k=KT)
        xs = carve(WB, 16384, KT * TB)
        wo = carve(ACC, 36864, 2 * KT * HID, F16).rearrange("p (h k n) -> p h k n", h=2, k=KT)
        ang = carve(WB, 24576, 2 * TT * AW)
        v = carve(WB, 36864, TT * KVW).rearrange("p (t n) -> p t n", t=TT)
        xtile = carve(WB, 40960, TT * HID).rearrange("p (t n) -> p t n", t=TT)
        ring = carve(ACC, 0, QK * 3 * TB).rearrange("p (s c n) -> p s c n", s=QK, c=3)
        dif = [carve(ACC, 45056 + 4096 * n, HH * KV_HEADS * E) for n in range(2)]
        prod = [carve(ACC, 53248, HH * D * KV_HEADS), carve(DQ, 0, HH * D * KV_HEADS)]
        wraw = carve(ACC, 0, KT * QKV).rearrange("p (k n) -> p k n", k=KT)
        woraw = carve(ACC, 45056, KT * HID).rearrange("p (k n) -> p k n", k=KT)
        cst = carve(T2, 0, C_END)
        rdir = carve(T2, 1600, 2 * 4 * E).rearrange("p (c n) -> p c n", c=2)
        bv = carve(T2, 2112, KVW)
        tab = carve(T2, 3136, 2 * TB).rearrange("p (c n) -> p c n", c=2)
        small = carve(T2, 7232, 128)
        oT = carve(T2, 7744, 2 * 2 * KT * P, F16).rearrange("p (b s k n) -> p b s k n", b=2, s=2, k=KT)
        score = carve(T2, 11840, 2 * HH * KV_HEADS).rearrange("p (b n) -> p b n", b=2)
        turns = carve(T2, 12352, AW)
        o = [carve(t, at, TT * HH * D).rearrange("p (h t d) -> p h t d", h=HH, t=TT) for t, at in ((T2, 13888), (ACC, 61440))]
        bo = carve(DQ, 8192, HID)
        bo_halves = carve(T2, 17984, 2 * HID + P, F16)
        gbuf = carve(T2, 0, 2 * TB).rearrange("p (b n) -> p b n", b=2)
        zbuf = carve(T2, 4096, 2 * TB).rearrange("p (b n) -> p b n", b=2)
        inter = carve(T2, 8192, 4 * 2 * TB // 2).bitcast(F16).rearrange("p (s h n) -> p s h n", s=4, h=2)
        stat = carve(T2, 16384, 64)
        raw, first_raw = carve(DQ, 0, UC, I32), carve(ACC, 0, UNITS * UC, I32)
        scl, first_scl = carve(DQ, 1536, UC), carve(ACC, 12288, UNITS * UC)
        c16, first_c16 = carve(DQ, 3072, UC, U16), carve(ACC, 24576, 2 * UC, U16)
        mag, first_mag = carve(DQ, 3840, UC, U16), carve(ACC, 26112, UC, U16)
        sgn, first_sgn = carve(DQ, 4608, UC, U16), carve(ACC, 26880, UC, U16)
        w32, first_w32 = carve(DQ, 5376, UC), carve(ACC, 27648, 4 * UC)

        def in_first_chunk(u):
            return isinstance(u, int) and u < UNITS

        def code_buffers(u):
            if not in_first_chunk(u):
                return raw, scl, c16
            mine = slice(u * UC, (u + 1) * UC)
            return first_raw[:, mine], first_scl[:, mine], first_c16[:, u % 2 * UC:(u % 2 + 1) * UC]

        def weight_buffer(u, nib):
            at = (2 * (u % 2) + nib) * UC if in_first_chunk(u) else 0
            return first_w32[:, at:at + UC] if in_first_chunk(u) else w32

        total = carve(DQ, 0, TT * HID).rearrange("p (t n) -> p t n", t=TT)

        ident = cst[:, C_IDENT:C_IDENT + P]
        norms = small[:, 64:112].rearrange("p (b n) -> p b n", b=2)
        ln_eps, biases, scratch = small[:, 112:113], small[:, 113:119], small[:, 120:121]

        def stats(tt):
            return small[:, 16 * tt:16 * tt + 16]

        def product_operands(u):
            shape = [P, HH, D, KV_HEADS]
            return (prod[u % 2].rearrange("p (h d g) -> p h d g", h=HH, g=KV_HEADS),
                    score[:, u % 2, :].rearrange("p (h g) -> p h g", g=KV_HEADS).unsqueeze(2).to_broadcast(shape),
                    v[:, u % TT, :].rearrange("p (g d) -> p d g", d=D).unsqueeze(1).to_broadcast(shape))

        x1_d = nc.dram_tensor("x1_scratch", (TT, 2 + BLOCKS, P, HID), F32).ap()

        bank = [ctx.enter_context(nc.psum_tensor(f"bank{b}", [P, 512], F32))[:, :] for b in range(8)]
        job, feat, otp, att, trp = bank[0:JB], bank[3:5], bank[5], bank[6], bank[7]
        gate, up, down = bank[0:2], bank[2:4], bank[4:8]

        constants_loaded = sem("constants_loaded")
        wraw_loaded = [sem(f"wraw_loaded_{k}") for k in range(KT)]
        woraw_loaded = sem("woraw_loaded")
        wqkv_hi = sem("wqkv_hi")
        wqkv_lo = sem("wqkv_lo")
        prepared = sem("prepared")
        bo_hi = sem("bo_hi")
        wo_hi = sem("wo_hi")
        wo_lo = sem("wo_lo")
        x_loaded = sem("x_loaded")
        x_hi = sem("x_hi")
        x_lo = sem("x_lo")
        tab_loaded = sem("tab_loaded")
        job_ready = sem("job_ready")
        job_used = sem("job_used")
        squared = sem("squared")
        feat_ready = sem("feat_ready")
        norm_ready = sem("norm_ready")
        feat_used = sem("feat_used")
        ang_ready = sem("ang_ready")
        dif_ready = sem("dif_ready")
        sin_ready = sem("sin_ready")
        sin2_ready = sem("sin2_ready")
        score_ready = sem("score_ready")
        prod_ready = sem("prod_ready")
        o_ready = sem("o_ready")
        ot_ready = sem("ot_ready")
        ot_hi = sem("ot_hi")
        ot_lo = sem("ot_lo")
        xtile_loaded = [sem(f"xtile_loaded_{tt}") for tt in range(TT)]
        att_ready = sem("att_ready")
        y_ready = sem("y_ready")
        moments_taken = sem("moments_taken")
        var_ready = sem("var_ready")
        std_ready = sem("std_ready")
        inverse_ready = sem("inverse_ready")
        shift_ready = sem("shift_ready")
        x1_ready = sem("x1_ready")
        x1_stored = [sem(f"x1_stored_{tt}") for tt in range(TT)]
        acc_loaded = sem("acc_loaded")
        tr_ready = sem("tr_ready")
        x1_hi = sem("x1_hi")
        x1_lo = sem("x1_lo")
        first_loaded = sem("first_chunk_loaded")
        codes_loaded = sem("codes_loaded")
        scales_loaded = sem("scales_loaded")
        c16_ready = sem("c16_ready")
        w32_ready = sem("w32_ready")
        weight_hi = sem("weight_hi")
        weight_lo = sem("weight_lo")
        gate_ready = sem("gate_ready")
        gate_copied = sem("gate_copied")
        gate_squared = sem("gate_squared")
        z_ready = sem("z_ready")
        tanh_ready = sem("tanh_ready")
        up_ready = sem("up_ready")
        inter_ready = sem("inter_ready")
        inter_hi = sem("inter_hi")
        inter_lo = sem("inter_lo")
        down_ready = sem("down_ready")
        down_added = sem("down_added")
        out_ready = sem("out_ready")
        out_written = sem("out_written")
        vector_prod_ready = sem("vector_product_ready")
        own_early = sem("vector_own_early")
        own_late = sem("vector_own_late")
        own_dq = sem("vector_own_dequant")
        own_ffn = sem("vector_own_ffn")
        own_ln = sem("vector_own_layernorm")
        OWN_EARLY, OWN_LATE, OWN_DQ, OWN_FFN, OWN_LN = 3 * TT, UPB, 6, 2 * NT, 20

        block = ctx.enter_context(nc.Block())

        def ge(eng, semaphore, value):
            if not isinstance(value, int) or value > 0:
                eng.wait_ge(semaphore, value)

        def pool_products(b, u):
            return b * (UPB - 1) + (u + 1) - (1 if u >= VU else 0)

        def attention_blocks(eng, body):
            body(0, None, None, True)
            body(1, 0, None, True)
            with eng.Fori(2, BLOCKS - 1) as i:
                body(i, i - 1, i - 2, True)
            body(BLOCKS - 1, BLOCKS - 2, BLOCKS - 3, False)
            body(None, BLOCKS - 1, BLOCKS - 2, False)
            body(None, None, BLOCKS - 1, False)

        def in_order(order, first, second, i, b, c, after=None):
            for step, n in order:
                at = i if step in first else b if step in second or n < 2 else c
                if at is not None:
                    step(at, n)
                if after:
                    after(step, n)

        def ffn_steps(eng, body, before_sums=None):
            body(0, False, True, False)
            if before_sums:
                before_sums()
            with eng.Fori(1, STEPS - BLOCKS) as g:
                body(g, True, True, False)
            body(STEPS - BLOCKS, True, False, False)
            body(STEPS - BLOCKS + 1, True, False, True)
            with eng.Fori(STEPS - BLOCKS + 2, STEPS) as g:
                body(g, True, False, True)

        @block.sync
        def _(sp):
            for k in range(KT):
                sp.dma_start(wraw[:, k, :], wqkv_d[:, k * QKV:(k + 1) * QKV]).then_inc(wraw_loaded[k], 16)
            sp.dma_start(cst, consts_d).then_inc(constants_loaded, 16)
            sp.dma_start(rdir.rearrange("p c n -> p (c n)"), r_d).then_inc(constants_loaded, 16)
            sp.dma_start(bv, bv_d.partition_broadcast(P)).then_inc(constants_loaded, 16)
            sp.dma_start(bo, bo_d.partition_broadcast(P)).then_inc(constants_loaded, 16)

            def one(blocks, i):
                if isinstance(i, int):
                    return blocks[i]
                return blocks[ds(i, 1)].rearrange("o p n -> (o p) n")

            def load_x(i, shift=0):
                ge(sp, x_lo, i + shift)
                sp.dma_start(xs, one(xblk[shift:], i)).then_inc(x_loaded, 16)

            def load_table(i, shift=0):
                ge(sp, job_used, len(JOBS) * (i + (shift - 1)) + QK)
                sp.dma_start(tab.rearrange("p c n -> p (c n)"), one(tables_d[shift:], i)).then_inc(tab_loaded, 16)

            def load_tile(i, tt):
                sp.dma_start(xtile[:, tt, :], one(x[LOAD_ORDER.index(tt)], i)).then_inc(
                    xtile_loaded[tt], 16)

            load_x(0)
            load_table(0)
            sp.dma_start(woraw.rearrange("p k n -> p (k n)"), wo_d).then_inc(woraw_loaded, 16)
            for tt in range(TT):
                load_tile(0, tt)

            def store_x1(b, tt, at):
                sp.wait_ge(tr_ready, b * TT + (tt + 1))
                sp.dma_start(at, xtile[:, tt, :]).then_inc(x1_stored[tt], 16)

            def body(i, b, c, following):
                if following:
                    load_x(i, 1)
                if i is None and b is not None:
                    sp.wait_ge(feat_ready, TILES)
                    for buffer, array in ((first_raw, codes_d), (first_scl, scales_d)):
                        sp.dma_start(buffer.rearrange("p (u n) -> p u n", u=UNITS),
                                     array[0:UNITS].rearrange("u p n -> p u n")).then_inc(first_loaded, 16)
                for tt in (2, 3):
                    if c is not None:
                        store_x1(c, tt, one(x1_d[tt], i) if i is not None else x1_d[tt, 2 + c])
                        if b is not None:
                            sp.wait_ge(x1_stored[tt], 16 * (c + 1))
                            load_tile(b, tt)
                    if following and tt == 2:
                        load_table(i, 1)
                if b is not None:
                    for tt in (0, 1):
                        store_x1(b, tt, one(x1_d[tt, 1:], i) if i is not None else x1_d[tt, 2 + b])
                        if i is not None:
                            sp.wait_ge(x1_stored[tt], 16 * (b + 1))
                            load_tile(i, tt)

            attention_blocks(sp, body)

            def load_codes(u):
                sp.wait_ge(c16_ready, u)
                sp.dma_start(raw, codes_d[ds(u, 1), :, :].rearrange("o p n -> (o p) n")).then_inc(codes_loaded, 16)
                sp.wait_ge(w32_ready, 2 * u)
                sp.dma_start(scl, scales_d[ds(u, 1), :, :].rearrange("o p n -> (o p) n")).then_inc(scales_loaded, 16)

            sp.wait_ge(o_ready, BLOCKS * UPB)
            sp.wait_ge(weight_lo, 2 * UNITS)
            sp.wait_ge(x1_lo, TILES)
            for tt in range(TT):
                sp.wait_ge(x1_stored[tt], 16 * BLOCKS)
            with sp.Fori(0, BLOCKS) as b:
                sp.dma_start(ACC[:, ds(b * (TT * HID), TT * HID)].rearrange("p (t n) -> p t n", t=TT),
                             x1_d[:, 2:][:, ds(b, 1)].rearrange("t o p n -> p (o t) n")).then_inc(acc_loaded, 16)
            with sp.Fori(UNITS, CHUNKS * UNITS) as u:
                load_codes(u)

            with sp.Fori(0, BLOCKS) as b:
                for tt in range(TT):
                    sp.wait_ge(out_ready, b * TT + (tt + 1))
                    sp.dma_start(out[ds(b * TB + tt * P, P), :], total[:, tt, :]).then_inc(out_written, 16)
            sp.wait_ge(out_written, 16 * TILES)

        @block.gpsimd
        def _(pool):
            def difference(b, u):
                n, tt, half = b * UPB + u, u % TT, u // TT
                if u == 0:
                    pool.wait_ge(ang_ready, (b + 1) * TT)
                ge(pool, score_ready, n - 1)
                at = (b & 1) * (TT * AW) + tt * AW
                q = ang[:, ds(at + (KV_HEADS + half * HH) * E, HH * E)]
                k = ang[:, ds(at, KV_HEADS * E)]
                shape = [P, HH, KV_HEADS, E]
                nc.gpsimd.tensor_tensor(
                    dif[u % 2].rearrange("p (h g e) -> p h g e", h=HH, g=KV_HEADS),
                    q.rearrange("p (h e) -> p h e", e=E).unsqueeze(2).to_broadcast(shape),
                    k.rearrange("p (g e) -> p g e", e=E).unsqueeze(1).to_broadcast(shape),
                    ALU.subtract).then_inc(dif_ready, 1)

            def product(b, u):
                n = b * UPB + u
                if u == 0:
                    pool.wait_ge(job_used, (b + 1) * len(JOBS))
                ge(pool, o_ready, n - 1)
                pool.wait_ge(score_ready, n + 1)
                nc.gpsimd.tensor_tensor(*product_operands(u), ALU.mult).then_inc(prod_ready, 1)

            def weight_lo_half(u, nib):
                pool.wait_ge(weight_hi, 2 * u + (nib + 1))
                par = ((u >> 3) & 1) * WPAR
                col = nib * 2 * WCH
                at = par + (u & 7) * UC
                nc.gpsimd.tensor_tensor(WB[:, ds(at + (col + WCH), UC)], weight_buffer(u, nib), WB[:, ds(at + col, UC)],
                                        ALU.subtract).then_inc(weight_lo, 1)

            def first_chunk(step, n):
                if (step, n) in ORDER_LO:
                    weight_lo_half(ORDER_LO.index((step, n)), 0)
                    weight_lo_half(ORDER_LO.index((step, n)), 1)

            ORDER_LO = ((product, 2), (difference, 5), (product, 4), (product, 5), (product, 6))
            POOL_ORDER = (
                (difference, 0), (difference, 1), (product, 0), (difference, 2), (difference, 3), (product, 1),
                (difference, 4), (product, 2), (difference, 5), (difference, 6), (product, 4), (difference, 7),
                (product, 5), (product, 6), (product, 7))

            def body(i, b, c, following):
                if b is not None:
                    in_order(POOL_ORDER, (), (difference, product), i, b, c, first_chunk if i is None else None)
                    if i is None:
                        for u in range(UNITS - 3, UNITS):
                            weight_lo_half(u, 0)
                            weight_lo_half(u, 1)

            pool.wait_ge(wo_lo, KT)
            attention_blocks(pool, body)

            def body(g, add, dequantise, normalise):
                for nt in range(NT):
                    pool.wait_ge(inter_hi, g * NT + (nt + 1))
                    nc.gpsimd.tensor_tensor(inter[:, nt, 1, :], zbuf[:, nt % 2, :], inter[:, nt, 0, :],
                                            ALU.subtract).then_inc(inter_lo, 1)
                    if dequantise and nt >= 2:
                        weight_lo_half(g + UNITS, nt - 2)

            ffn_steps(pool, body)

        @block.scalar
        def _(act):
            for k in range(KT):
                act.wait_ge(wraw_loaded[k], 16)
                nc.scalar.activation(wqkv[:, 0, k, :], wraw[:, k, :], ACT.Copy, scale=W_SCALE).then_inc(wqkv_hi, 1)

            def split_hi(i, n=0):
                act.wait_ge(x_loaded, 16 * (i + 1))
                nc.scalar.activation(XT[:, ds(i * XB, KT * TB)], xs, ACT.Copy).then_inc(x_hi, 1)

            split_hi(0)
            for k in range(KT):
                act.wait_ge(woraw_loaded, 16)
                nc.scalar.activation(wo[:, 0, k, :], woraw[:, k, :], ACT.Copy, scale=W_SCALE).then_inc(wo_hi, 1)
            act.wait_ge(prepared, 1)

            def square(i, k):
                act.wait_ge(job_ready, i * len(JOBS) + (k + 1))
                ge(act, feat_ready, i * TT)
                nc.scalar.activation(ring[:, k, 2, :], job[k % JB], ACT.Square,
                                     bias=biases[:, k:k + 1]).then_inc(squared, 1)

            def sine(b, u):
                n = b * UPB + (u + 1)
                act.wait_ge(dif_ready, n)
                nc.scalar.activation(dif[u % 2], dif[u % 2], ACT.Sin, scale=HALF_TURN).then_inc(sin_ready, 1)
                act.wait_ge(sin_ready, n)
                nc.scalar.activation(dif[u % 2], dif[u % 2], ACT.Square).then_inc(sin2_ready, 1)

            def turned_hi(b, tt):
                t = b * TT + tt
                act.wait_ge(ot_ready, t + 1)
                ge(act, att_ready, t - 1)
                nc.scalar.activation(oT[:, tt % 2, 0, :, :].rearrange("p k n -> p (k n)"), otp, ACT.Copy,
                                     scale=O_SCALE).then_inc(ot_hi, 1)

            def deviation(b, tt):
                act.wait_ge(var_ready, b * TT + (tt + 1))
                nc.scalar.activation(stats(tt)[:, 8:9], stats(tt)[:, 7:8], ACT.Sqrt, bias=ln_eps).then_inc(std_ready, 1)

            def shift(b, tt):
                act.wait_ge(shift_ready, b * TT + (tt + 1))
                nc.scalar.activation(xtile[:, tt, :], xtile[:, tt, :], ACT.Identity, bias=stats(tt)[:, 10:11],
                                     scale=stats(tt)[:, 9:10]).then_inc(x1_ready, 1)

            def keep_hi(b, tt):
                act.wait_ge(tr_ready, b * TT + (tt + 1))
                nc.scalar.activation(xt_half(b, 0)[:, :, tt * P:tt * P + P],
                                     trp.rearrange("p (k n) -> p k n", k=KT), ACT.Copy,
                                     scale=X1_SCALE).then_inc(x1_hi, 1)

            def root(i, tt):
                act.wait_ge(feat_ready, i * TT + (tt + 1))
                ge(act, feat_used, i * TT + (tt - 1))
                nc.scalar.activation(norms[:, tt % 2, :], feat[tt % 2][:, AW:AW + KV_HEADS + HEADS],
                                     ACT.Sqrt).then_inc(norm_ready, 1)

            def split_next(i, n):
                split_hi(i + 1)

            def narrow(u):
                raw, _, c16 = code_buffers(u)
                if in_first_chunk(u):
                    act.wait_ge(first_loaded, 2 * 16)
                    ge(act, w32_ready, 2 * (u - 1))
                else:
                    act.wait_ge(codes_loaded, 16 * (u - (UNITS - 1)))
                    act.wait_ge(w32_ready, 2 * u)
                nc.scalar.activation(c16, raw.bitcast(U16).rearrange("p (n two) -> p n two", two=2)[:, :, 0],
                                     ACT.Copy).then_inc(c16_ready, 1)

            def weight_hi_half(u, nib):
                act.wait_ge(w32_ready, 2 * u + (nib + 1))
                at = ((u >> 3) & 1) * WPAR + (u & 7) * UC + nib * 2 * WCH
                nc.scalar.activation(WB[:, ds(at, UC)], weight_buffer(u, nib), ACT.Copy).then_inc(weight_hi, 1)

            def first_chunk(step, n):
                if step is sine and n >= 1:
                    narrow(n - 1)
                if step is sine and n >= 3:
                    weight_hi_half(n - 3, 0)
                    weight_hi_half(n - 3, 1)

            SCALAR_ORDER = (
                (sine, 0), (square, 0), (square, 1), (turned_hi, 2), (sine, 1), (square, 2), (square, 3),
                (square, 4), (sine, 2), (square, 5), (split_next, 0), (turned_hi, 3), (sine, 3), (sine, 4),
                (deviation, 2), (root, 0), (sine, 5), (shift, 2), (keep_hi, 2), (root, 1), (sine, 6),
                (turned_hi, 0), (root, 2), (deviation, 3), (sine, 7), (turned_hi, 1), (shift, 3), (deviation, 0),
                (root, 3), (keep_hi, 3), (shift, 0), (deviation, 1), (keep_hi, 0), (shift, 1), (keep_hi, 1))

            def body(i, b, c, following):
                order = SCALAR_ORDER if following else [s for s in SCALAR_ORDER if s[0] is not split_next]
                first = i is None and b is not None
                if first:
                    act.wait_ge(job_ready, BLOCKS * len(JOBS))
                    act.wait_ge(x_lo, BLOCKS)
                in_order(order, (square, root, split_next), (sine,), i, b, c, first_chunk if first else None)
                if first:
                    narrow(UNITS - 1)
                    for u in range(UNITS - 3, UNITS):
                        weight_hi_half(u, 0)
                        weight_hi_half(u, 1)

            attention_blocks(act, body)

            def body(g, add, dequantise, normalise):
                for nt in range(NT):
                    b = nt % 2
                    act.wait_ge(gate_ready, g * NT + (nt + 1))
                    ge(act, inter_ready, g * NT + (nt - 1))
                    ge(act, inter_lo, g * NT + (nt - 1))
                    nc.scalar.activation(gbuf[:, b, :], gate[b], ACT.Copy,
                                         scale=1.0 / (X1_SCALE * FFN_SCALE)).then_inc(gate_copied, 1)
                    nc.scalar.activation(zbuf[:, b, :], gate[b], ACT.Square,
                                         scale=1.0 / (X1_SCALE * FFN_SCALE)).then_inc(gate_squared, 1)
                    act.wait_ge(z_ready, g * NT + (nt + 1))
                    nc.scalar.activation(zbuf[:, b, :], zbuf[:, b, :], ACT.Tanh, scale=GELU_C).then_inc(tanh_ready, 1)
                    act.wait_ge(inter_ready, g * NT + (nt + 1))
                    if not isinstance(g, int) or g > 0:
                        act.wait_ge(down_ready, g * NT * TT + (nt - NT + 1) * TT)
                    nc.scalar.activation(inter[:, nt, 0, :], zbuf[:, b, :], ACT.Copy).then_inc(inter_hi, 1)
                    if dequantise and nt == 1:
                        narrow(g + UNITS)
                    if dequantise and nt >= 2:
                        if nt == 2:
                            ge(act, down_ready, g * (NT * TT))
                        weight_hi_half(g + UNITS, nt - 2)

            ffn_steps(act, body)

        @block.vector
        def _(dve):
            def split_lo(i):
                dve.wait_ge(x_hi, i + 1)
                nc.vector.tensor_tensor(XT[:, ds(i * XB + KT * TB, KT * TB)], xs, XT[:, ds(i * XB, KT * TB)],
                                        ALU.subtract).then_inc(x_lo, 1)

            for k in range(KT):
                dve.wait_ge(wqkv_hi, k + 1)
                nc.vector.scalar_tensor_tensor(wqkv[:, 1, k, :], wraw[:, k, :], W_SCALE, wqkv[:, 0, k, :],
                                               ALU.mult, ALU.subtract).then_inc(wqkv_lo, 1)
            dve.wait_ge(constants_loaded, 16 * 4)
            nc.vector.memset(ln_eps, LN_EPS)
            nc.vector.tensor_scalar(rdir[:, 1, :], rdir[:, 1, :], cst[:, C_SIGN:C_SIGN + 1], None, ALU.mult)
            nc.vector.tensor_scalar(biases, cst[:, C_BIAS:C_BIAS + 6], W_SCALE, None, ALU.mult).then_inc(prepared, 1)
            split_lo(0)
            nc.vector.memset(bo_halves[0:1, 2 * HID:], O_SCALE * W_SCALE / BO_SCALE)
            nc.vector.tensor_scalar(bo_halves[0:1, 0:HID], bo[0:1, :], BO_SCALE, None, ALU.mult).then_inc(bo_hi, 1)
            dve.wait_ge(bo_hi, 1)
            nc.vector.scalar_tensor_tensor(bo_halves[0:1, HID:2 * HID], bo[0:1, :], BO_SCALE, bo_halves[0:1, 0:HID],
                                           ALU.mult, ALU.subtract)
            for k in range(KT):
                dve.wait_ge(wo_hi, k + 1)
                nc.vector.scalar_tensor_tensor(wo[:, 1, k, :], woraw[:, k, :], W_SCALE, wo[:, 0, k, :],
                                               ALU.mult, ALU.subtract).then_inc(wo_lo, 1)
            dve.wait_ge(prepared, 1)
            dve.wait_ge(wqkv_lo, KT)

            def rotate(i, k, own):
                if k == 0:
                    dve.wait_ge(tab_loaded, 16 * (i + 1))
                dve.wait_ge(squared, i * QK + (k + 1))
                ge(dve, feat_ready, i * TT)
                for c in range(2):
                    last = nc.vector.scalar_tensor_tensor(ring[:, k, c, :], job[k % JB], biases[:, k:k + 1],
                                                          tab[:, c, :], ALU.add, ALU.mult)
                last.then_inc(job_used, 1)

            def value(i, pair, own):
                k = QK + pair
                dve.wait_ge(job_ready, i * len(JOBS) + (k + 1))
                ge(dve, prod_ready, pool_products(i, -1 - 2 * (1 - pair)))
                nc.vector.scalar_tensor_tensor(
                    v[:, 2 * pair:2 * pair + 2, :], job[k % JB].rearrange("p (t n) -> p t n", t=2), 1.0 / W_SCALE,
                    bv.unsqueeze(1).to_broadcast([P, 2, KVW]), ALU.mult, ALU.add).then_inc(job_used, 1)

            def normalise(i, tt, own):
                dve.wait_ge(norm_ready, i * TT + (tt + 1))
                r = norms[:, tt % 2, :]
                own.done(nc.vector.tensor_scalar(r, r, NORM_EPS * W_SCALE, TWO_PI, ALU.max, ALU.mult))
                own.done(nc.vector.reciprocal(r, r))
                if tt == 0:
                    ge(dve, dif_ready, (i - 1) * UPB)
                mine = ang[:, ds((i & 1) * (TT * AW) + tt * AW, AW)]
                nc.vector.tensor_tensor(
                    mine.rearrange("p (h e) -> p h e", e=E),
                    feat[tt % 2][:, 0:AW].rearrange("p (h e) -> p h e", e=E),
                    r.unsqueeze(2).to_broadcast([P, KV_HEADS + HEADS, E]), ALU.mult).then_inc(feat_used, 1)
                dve.wait_ge(feat_used, i * TT + (tt + 1))
                own.done(nc.vector.tensor_scalar(turns, mine, ROUND, None, ALU.add))
                nc.vector.scalar_tensor_tensor(mine, turns, ROUND, mine, ALU.subtract, ALU.subtract).then_inc(ang_ready, 1)

            def scores(b, u, own):
                n = b * UPB + u
                dve.wait_ge(sin2_ready, n + 1)
                if u - 2 == VU:
                    dve.wait_ge(vector_prod_ready, b + 1)
                else:
                    ge(dve, prod_ready, pool_products(b, u - 2))
                own.done(nc.vector.tensor_reduce(score[:, u % 2, :], dif[u % 2].rearrange("p (n e) -> p n e", e=E),
                                                 AX.X, ALU.add))
                nc.vector.tensor_scalar(score[:, u % 2, :], score[:, u % 2, :], -2.0 * GROUP / D, GROUP * E / D,
                                        ALU.mult, ALU.add).then_inc(score_ready, 1)

            def product(b, u, own):
                n = b * UPB + u
                ge(dve, o_ready, n - 1)
                dve.wait_ge(score_ready, n + 1)
                nc.vector.tensor_tensor(*product_operands(u), ALU.mult).then_inc(vector_prod_ready, 1)

            def sum_heads(b, u, own):
                n, tt, half = b * UPB + u, u % TT, u // TT
                if u == VU:
                    dve.wait_ge(vector_prod_ready, b + 1)
                else:
                    dve.wait_ge(prod_ready, pool_products(b, u))
                ge(dve, ot_ready, b * TT - 2 * (1 - half))
                nc.vector.tensor_reduce(o[half][:, :, tt, :],
                                        prod[u % 2].rearrange("p (h d g) -> p h d g", h=HH, g=KV_HEADS),
                                        AX.X, ALU.add).then_inc(o_ready, 1)

            def turned_lo(b, tt, own):
                dve.wait_ge(ot_hi, b * TT + (tt + 1))
                nc.vector.scalar_tensor_tensor(oT[:, tt % 2, 1, :, :].rearrange("p k n -> p (k n)"), otp, O_SCALE,
                                               oT[:, tt % 2, 0, :, :].rearrange("p k n -> p (k n)"),
                                               ALU.mult, ALU.subtract).then_inc(ot_lo, 1)

            def moments(b, tt, own):
                t1 = b * TT + (tt + 1)
                dve.wait_ge(xtile_loaded[tt], 16 * (b + 1))
                dve.wait_ge(att_ready, t1)
                nc.vector.scalar_tensor_tensor(xtile[:, tt, :], att, 1.0 / (O_SCALE * W_SCALE), xtile[:, tt, :],
                                               ALU.mult, ALU.add).then_inc(y_ready, 1)
                dve.wait_ge(y_ready, t1)
                nc.vector.bn_stats(stats(tt)[:, 0:6], xtile[:, tt, :]).then_inc(moments_taken, 1)
                dve.wait_ge(moments_taken, t1)
                nc.vector.memset(scratch, 0.0)
                nc.vector.bn_aggr(stats(tt)[:, 6:8], stats(tt)[:, 0:6]).then_inc(var_ready, 1)

            def inverse(b, tt, own):
                t1 = b * TT + (tt + 1)
                dve.wait_ge(std_ready, t1)
                nc.vector.reciprocal(stats(tt)[:, 9:10], stats(tt)[:, 8:9]).then_inc(inverse_ready, 1)
                dve.wait_ge(inverse_ready, t1)
                nc.vector.scalar_tensor_tensor(stats(tt)[:, 10:11], stats(tt)[:, 6:7], -1.0, stats(tt)[:, 9:10],
                                               ALU.mult, ALU.mult).then_inc(shift_ready, 1)

            def keep_lo(b, tt, own):
                dve.wait_ge(x1_hi, b * TT + (tt + 1))
                nc.vector.scalar_tensor_tensor(
                    xt_half(b, 1)[:, :, tt * P:tt * P + P], trp.rearrange("p (k n) -> p k n", k=KT), X1_SCALE,
                    xt_half(b, 0)[:, :, tt * P:tt * P + P], ALU.mult, ALU.subtract).then_inc(x1_lo, 1)

            def split_next(i, n, own):
                split_lo(i + 1)

            def scaled(u, nib, own):
                _, scl, c16 = code_buffers(u)
                first = in_first_chunk(u)
                mag_, sgn_ = (first_mag, first_sgn) if first else (mag, sgn)
                if nib == 0:
                    dve.wait_ge(c16_ready, u + 1)
                ge(dve, w32_ready, 2 * u + nib)
                shift = 9 - 4 * nib
                own.done(nc.vector.tensor_scalar(mag_, c16, shift, 0x0E00, ALU.logical_shift_left, ALU.bitwise_and))
                own.done(nc.vector.tensor_scalar(sgn_, c16, shift + 3, 0x8000, ALU.logical_shift_left, ALU.bitwise_and))
                own.done(nc.vector.tensor_tensor(mag_, mag_, sgn_, ALU.bitwise_or))
                if first:
                    ge(dve, weight_lo, 2 * u + nib - 3)
                else:
                    dve.wait_ge(scales_loaded, 16 * (u - (UNITS - 1)))
                    dve.wait_ge(weight_lo, 2 * u + nib)
                nc.vector.scalar_tensor_tensor(weight_buffer(u, nib), mag_.bitcast(F16), FP4_BITS * FFN_SCALE, scl,
                                               ALU.mult, ALU.mult).then_inc(w32_ready, 1)

            VECTOR_ORDER = (
                (scores, 0), (rotate, 0), (rotate, 1), (turned_lo, 2), (rotate, 2), (scores, 1), (rotate, 3),
                (sum_heads, 0), (rotate, 4), (scores, 2), (rotate, 5), (turned_lo, 3), (split_next, 0),
                (moments, 2), (scores, 3), (sum_heads, 1), (product, 3), (inverse, 2), (normalise, 0), (scores, 4),
                (sum_heads, 2), (sum_heads, 3), (moments, 3), (normalise, 1), (scores, 5), (turned_lo, 0),
                (scores, 6), (inverse, 3), (normalise, 2), (keep_lo, 2), (sum_heads, 4), (moments, 0),
                (turned_lo, 1), (scores, 7), (sum_heads, 5), (keep_lo, 3), (inverse, 0), (moments, 1), (value, 0),
                (inverse, 1), (keep_lo, 0), (normalise, 3), (sum_heads, 6), (value, 1), (sum_heads, 7),
                (keep_lo, 1))

            def body(i, b, c, following):
                early = Own(dve, own_early, 0 if i is None else i * OWN_EARLY)
                late = Own(dve, own_late, 0 if b is None else b * OWN_LATE)
                for step, n in VECTOR_ORDER:
                    if step is split_next and not following:
                        continue
                    if step in (rotate, value, normalise, split_next):
                        if i is not None:
                            step(i, n, early)
                    elif step in (scores, sum_heads, product) or n < 2:
                        if b is not None:
                            step(b, n, late)
                        if step is sum_heads and i is None and b is not None:
                            own = Own(dve, own_dq, n * OWN_DQ)
                            scaled(n, 0, own)
                            scaled(n, 1, own)
                    elif c is not None:
                        step(c, n, late)
                assert i is None or early.n == OWN_EARLY
                assert b is None or late.n == OWN_LATE

            attention_blocks(dve, body)

            def add_down(g, last):
                for tt in range(TT):
                    dve.wait_ge(down_ready, g * NT * TT + ((NT - 1) * TT + tt + 1))
                    if last:
                        ge(dve, out_written, ((g - (STEPS - BLOCKS)) * TT) * 16)
                    nc.vector.scalar_tensor_tensor(total[:, tt, :] if last else acc(g & (BLOCKS - 1), tt),
                                                   down[tt], 1.0 / (INTER_SCALE * FFN_SCALE),
                                                   acc(g & (BLOCKS - 1), tt), ALU.mult, ALU.add).then_inc(down_added, 1)

            def second_norm(g):
                own = Own(dve, own_ln, (g - (STEPS - BLOCKS)) * OWN_LN)
                dve.wait_ge(down_added, (g + 1) * TT)
                for tt in range(TT):
                    own.done(nc.vector.bn_stats(stat[:, 6 * tt:6 * tt + 6], total[:, tt, :]))
                nc.vector.memset(stat[:, 44:45], 0.0)
                for tt in range(TT):
                    ins = nc.vector.bn_aggr(stat[:, 24 + 2 * tt:26 + 2 * tt], stat[:, 6 * tt:6 * tt + 6])
                    own.tick(ins)
                own.wait()
                var = stat[:, 24:32].rearrange("p (t two) -> p t two", two=2)[:, :, 1]
                ve, y, t = stat[:, 32:36], stat[:, 36:40], stat[:, 40:44]
                own.done(nc.vector.tensor_scalar(ve, var, LN_EPS, None, ALU.add))
                own.done(nc.vector.tensor_scalar(t.bitcast(I32), ve.bitcast(I32), 1, None, ALU.logical_shift_right))
                own.done(nc.vector.tensor_scalar(y.bitcast(I32), t.bitcast(I32), -1.0, RSQRT_SEED, ALU.mult, ALU.add))
                for _ in range(3):
                    own.done(nc.vector.scalar_tensor_tensor(t, y, -0.5, y, ALU.mult, ALU.mult))
                    own.done(nc.vector.tensor_tensor(t, t, ve, ALU.mult))
                    own.done(nc.vector.scalar_tensor_tensor(y, t, 1.5, y, ALU.add, ALU.mult))
                for tt in range(TT):
                    nc.vector.tensor_scalar(total[:, tt, :], total[:, tt, :], stat[:, 24 + 2 * tt:25 + 2 * tt], y[:, tt:tt + 1],
                                            ALU.subtract, ALU.mult).then_inc(out_ready, 1)
                assert own.n == OWN_LN

            def body(g, add, dequantise, normalise):
                own = Own(dve, own_ffn, g * OWN_FFN)
                own_d = Own(dve, own_dq, (g + UNITS) * OWN_DQ)
                for nt in range(NT):
                    b = nt % 2
                    s1 = g * NT + (nt + 1)
                    dve.wait_ge(gate_squared, s1)
                    own.done(nc.vector.tensor_scalar(zbuf[:, b, :], zbuf[:, b, :], GELU_A, 1.0, ALU.mult, ALU.add))
                    nc.vector.tensor_tensor(zbuf[:, b, :], zbuf[:, b, :], gbuf[:, b, :], ALU.mult).then_inc(z_ready, 1)
                    dve.wait_ge(tanh_ready, s1)
                    own.done(nc.vector.scalar_tensor_tensor(gbuf[:, b, :], zbuf[:, b, :], 1.0, gbuf[:, b, :],
                                                            ALU.add, ALU.mult))
                    dve.wait_ge(up_ready, s1)
                    nc.vector.scalar_tensor_tensor(zbuf[:, b, :], up[b], 0.5 * INTER_SCALE / (X1_SCALE * FFN_SCALE),
                                                   gbuf[:, b, :], ALU.mult, ALU.mult).then_inc(inter_ready, 1)
                    if add and nt == 1:
                        add_down(g - 1, normalise)
                    if dequantise and nt in (1, 2):
                        scaled(g + UNITS, nt - 1, own_d)
                    if normalise and nt == 2:
                        second_norm(g - 1)
                assert own.n == OWN_FFN

            ffn_steps(dve, body, lambda: dve.wait_ge(acc_loaded, 16 * BLOCKS))
            add_down(STEPS - 1, True)
            second_norm(STEPS - 1)

        @block.tensor
        def _(pe):
            pe.wait_ge(prepared, 1)
            pe.wait_ge(wqkv_lo, KT)

            def free(i, k):
                ge(pe, job_used, i * len(JOBS) + ((k - JB + 1) if k >= JB else (-1, 0, -2)[k]))

            def project(i, k):
                _, col = JOBS[k]
                if k == 0:
                    pe.wait_ge(x_lo, i + 1)
                free(i, k)
                for kt in range(KT):
                    for a, b in HALVES:
                        last = nc.tensor.matmul(job[k % JB], wqkv[:, a, kt, col:col + P], xt(i, b, kt),
                                                start=(kt == 0 and a + b == 0), stop=(kt == KT - 1 and a == 1))
                last.then_inc(job_ready, 1)

            def project_v(i, pair):
                k = QK + pair
                _, col = JOBS[k]
                free(i, k)
                for t in range(2):
                    for kt in range(KT):
                        for a, b in HALVES:
                            last = nc.tensor.matmul(job[k % JB][:, t * KVW:(t + 1) * KVW],
                                                    xt(i, a, kt, (2 * pair + t) * P, P), wqkv[:, b, kt, col:col + KVW],
                                                    start=(kt == 0 and a + b == 0), stop=(kt == KT - 1 and a == 1))
                last.then_inc(job_ready, 1)

            def directions(i, tt):
                if tt == 0:
                    pe.wait_ge(job_used, i * len(JOBS) + QK)
                ge(pe, feat_used, i * TT + (tt - 1))
                bank_ = feat[tt % 2]
                for s in range(QK):
                    rows = slice(tt * P, (tt + 1) * P)
                    for c in range(2):
                        nc.tensor.matmul(bank_[:, s * 4 * E:(s + 1) * 4 * E], ring[:, s, c, rows], rdir[:, c, :],
                                         start=(c == 0), stop=(c == 1))
                    last = nc.tensor.matmul(bank_[:, AW + 4 * s:AW + 4 * s + 4], ring[:, s, 2, rows],
                                            cst[:, C_ONES4:C_ONES4 + 4], start=True, stop=True)
                last.then_inc(feat_ready, 1)

            def turn_o(b, tt):
                t = b * TT + tt
                pe.wait_ge(o_ready, b * UPB + TT * (1 + tt // 2))
                ge(pe, ot_lo, t)
                for h in range(KT):
                    last = nc.tensor.transpose(
                        otp.rearrange("p (k h j) -> p k h j", k=KT, h=KT)[:, :, h, :],
                        o[tt // 2][:, tt % 2 * KT + h, :, :].rearrange("p t d -> p (t d)"), ident)
                last.then_inc(ot_ready, 1)

            def project_o(b, tt):
                t = b * TT + tt
                pe.wait_ge(ot_lo, t + 1)
                ge(pe, y_ready, t)
                for kt in range(KT):
                    for a, h in HALVES:
                        nc.tensor.matmul(att, oT[:, tt % 2, a, kt, :], wo[:, h, kt, :],
                                         start=(kt == 0 and a + h == 0), stop=False)
                for half in range(2):
                    last = nc.tensor.matmul(att, bo_halves[0:1, 2 * HID:], bo_halves[0:1, half * HID:(half + 1) * HID],
                                            start=False, stop=half == 1)
                last.then_inc(att_ready, 1)

            def turn_x1(b, tt):
                t = b * TT + tt
                pe.wait_ge(x1_ready, t + 1)
                ge(pe, x1_lo, t)
                for kt in range(KT):
                    lo = (kt // 2) * 2 * P + kt % 2
                    last = nc.tensor.transpose(trp[:, kt * P:(kt + 1) * P], xtile[:, tt, lo:lo + 2 * P - 1:2], ident)
                last.then_inc(tr_ready, 1)

            TENSOR_ORDER = (
                (project, 0), (project, 1), (turn_o, 2), (project, 2), (project, 3), (project, 4), (project, 5),
                (turn_o, 3), (project_o, 2), (project_v, 0), (directions, 0), (project_o, 3), (directions, 1),
                (turn_x1, 2), (directions, 2), (turn_o, 0), (turn_o, 1), (project_o, 0), (directions, 3),
                (turn_x1, 3), (project_o, 1), (turn_x1, 0), (project_v, 1), (turn_x1, 1))

            def body(i, b, c, following):
                in_order(TENSOR_ORDER, (project, project_v, directions), (), i, b, c)

            attention_blocks(pe, body)
            pe.wait_ge(x1_lo, TILES)
            pe.wait_ge(feat_used, TILES)

            def hidden(ps, m, nt, par, b):
                for kt in range(KT):
                    for a, h in HALVES:
                        last = nc.tensor.matmul(ps, weight(par, m, kt, a, nt * P, P), xt(b, h, kt),
                                                start=(kt == 0 and a + h == 0), stop=(kt == KT - 1 and a == 1))
                return last

            def down_product(g, nt):
                b = g & (BLOCKS - 1)
                par = ((g >> 3) & 1) * WPAR
                if nt == 0:
                    pe.wait_ge(weight_lo, ((g >> 3) + 1) * (2 * UNITS))
                pe.wait_ge(inter_lo, g * NT + (nt + 1))
                for tt in range(TT):
                    if nt == 0:
                        ge(pe, down_added, g * TT + (tt - TT + 1))
                    for a, h in HALVES:
                        last = nc.tensor.matmul(down[tt], inter[:, nt, a, tt * P:(tt + 1) * P],
                                                weight(par, 2, nt, h, 0, HID),
                                                start=(nt == 0 and a + h == 0), stop=(nt == NT - 1 and a == 1))
                    last.then_inc(down_ready, 1)

            def body(g, add, dequantise, normalise):
                b = g & (BLOCKS - 1)
                par = ((g >> 3) & 1) * WPAR
                pe.wait_ge(weight_lo, (g >> 3) * (2 * UNITS) + 2 * HIDDEN_UNITS)
                for nt in range(NT):
                    s = g * NT + nt
                    ge(pe, gate_squared, s - 1)
                    hidden(gate[nt % 2], 0, nt, par, b).then_inc(gate_ready, 1)
                    ge(pe, inter_ready, s - 1)
                    hidden(up[nt % 2], 1, nt, par, b).then_inc(up_ready, 1)
                    if nt >= 2:
                        down_product(g, nt - 2)
                    elif add:
                        down_product(g - 1, nt + 2)

            ffn_steps(pe, body)
            down_product(STEPS - 1, 2)
            down_product(STEPS - 1, 3)


QUARTERS = BLOCKS // BATCH
ROWS_PH = SEQ // HEADS
ROW_SHAPE = (BATCH, TT, HEADS // TT, QUARTERS, ROWS_PH // QUARTERS, HID)


def by_token(a):
    n = a.shape[-1]
    return a.reshape(-1, TB // 16, 4, TT, n).transpose(0, 3, 2, 1, 4).reshape(-1, TB, n)


def host_constants():
    import numpy as np

    c = np.zeros((P, C_END), np.float32)
    c[:, C_IDENT:C_IDENT + P] = np.eye(P, dtype=np.float32)
    for h in range(4):
        c[D * h:D * h + D, C_ONES4 + h] = 1.0
    c[:, C_SIGN] = np.where(np.arange(P) % D < E, 1.0, -1.0)
    inv = np.float32(1.0) / np.power(np.float32(10000.0), np.arange(0, D, 2, dtype=np.float32) / np.float32(D))
    freqs = np.arange(SEQ, dtype=np.float32)[:, None] * inv.astype(np.float32)[None, :]
    emb = np.concatenate([freqs, freqs], axis=-1).astype(np.float64)
    emb = by_token(emb)
    tab = np.stack([np.cos(emb), np.sin(emb)]).astype(np.float32)
    tab = np.tile(tab.transpose(1, 3, 0, 2), (1, 4, 1, 1)).reshape(-1, P, 2 * TB)
    return c, np.concatenate([tab] * BATCH)


def kernel(**inputs):
    import numpy as np
    import concourse.bacc as bacc
    from concourse.bass_utils import run_bass_kernel_spmd

    a = {k.split("_", 1)[1]: np.asarray(val) for k, val in inputs.items()}
    x = a["attn_hidden_states"].reshape(TOKENS, HID)
    consts, tables = host_constants()
    consts[:, C_BIAS:C_BIAS + 2] = a["attn_bk"].reshape(2, P).T
    consts[:, C_BIAS + 2:C_BIAS + 6] = a["attn_bq"].reshape(4, P).T
    rt = a["attn_rand_matrix"].T
    rdir = np.zeros((P, 2, 4 * E), np.float32)
    for h in range(4):
        rdir[D * h:D * h + D, 0, h * E:(h + 1) * E] = rt
        rdir[D * h:D * h + D, 1, h * E:(h + 1) * E] = np.concatenate([rt[E:], rt[:E]])
    x_rows = x.reshape(ROW_SHAPE).transpose(1, 0, 3, 2, 4, 5).reshape(TT, BLOCKS, P, HID)[list(LOAD_ORDER)]
    wqkv = np.concatenate([a["attn_Wk"], a["attn_Wq"], a["attn_Wv"]])
    wqkv = wqkv.T.reshape(KT, P, QKV).transpose(1, 0, 2).reshape(P, KT * QKV)
    wo = a["attn_Wo"].T.reshape(KT, P, HID).transpose(1, 0, 2).reshape(P, KT * HID)
    xblk = by_token(x).transpose(0, 2, 1)
    xblk = xblk.reshape(BLOCKS, KT, P, TB).transpose(0, 2, 1, 3).reshape(BLOCKS, P, KT * TB)

    order = np.arange(CH).reshape(2, P, 2).transpose(0, 2, 1).reshape(CH)
    blocks_of = np.arange(2 * P).reshape(2, P) // E
    codes = np.empty((CHUNKS, P, 3, 2, CH), np.int32)
    scales = np.empty((CHUNKS, P, 3, 2, CH), np.float32)
    for c in range(CHUNKS):
        rows = c * CH + order
        for m, name in enumerate(("gate", "up")):
            codes[c, :, m] = a[f"ffn_{name}_W_packed"][rows].reshape(CH, 2, P).transpose(2, 1, 0)
            scales[c, :, m] = a[f"ffn_{name}_scales"][rows][:, blocks_of].transpose(2, 1, 0)
        cols = slice(c * 2 * P, (c + 1) * 2 * P)
        codes[c, :, 2] = a["ffn_down_W_packed"][:, cols].reshape(HID, 2, P).transpose(2, 1, 0)
        scales[c, :, 2] = a["ffn_down_scales"][:, c * CH // 32:][:, blocks_of].transpose(2, 1, 0)
    codes = codes.reshape(CHUNKS, P, UNITS, UC).transpose(0, 2, 1, 3).reshape(CHUNKS * UNITS, P, UC)
    scales = scales.reshape(CHUNKS, P, UNITS, UC).transpose(0, 2, 1, 3).reshape(CHUNKS * UNITS, P, UC)

    arrays = {"xblk": xblk, "x": x_rows, "wqkv": wqkv, "wo": wo, "rdir": rdir.reshape(P, 8 * E), "consts": consts,
              "bv": a["attn_bv"], "bo": a["attn_bo"], "tables": tables, "codes": codes, "scales": scales}
    arrays = {k: np.ascontiguousarray(val) for k, val in arrays.items()}
    nc = bacc.Bacc("TRN2", target_bir_lowering=False, num_devices=1)
    args = [nc.dram_tensor(k, val.shape, mybir.dt.from_np(val.dtype), kind="ExternalInput").ap()
            for k, val in arrays.items()]
    out = nc.dram_tensor("out", (TOKENS, HID), F32, kind="ExternalOutput").ap()
    build(nc, *args, out)
    r = run_bass_kernel_spmd(nc, [arrays], core_ids=[0])
    y = r.results[0]["out"].reshape(BATCH, QUARTERS, TT, HEADS // TT, ROWS_PH // QUARTERS, HID)
    return y.transpose(0, 2, 3, 1, 4, 5).reshape(BATCH, SEQ, HID)
```
